# Optimizing a Trainium2 kernel written in Bass

```python
import numpy as np
import jax
import jax.numpy as jnp

def _softmax(x, axis=-1):
    return jax.nn.softmax(x, axis=axis)

def _gelu(x):
    return jax.nn.gelu(x, approximate=True)

def _silu(x):
    return jax.nn.silu(x)

def _sigmoid(x):
    return jax.nn.sigmoid(x)

def _layernorm(x, axis=-1, eps=1e-05):
    m = jnp.mean(x, axis=axis, keepdims=True)
    v = jnp.var(x, axis=axis, keepdims=True)
    return (x - m) / jnp.sqrt(v + eps)

def _scatter_add(tgt, idx, src, axis=0):
    return tgt.at[idx].add(src)

def _segment_sum(src, seg, n):
    return jax.ops.segment_sum(src, seg, n)
kernel_name = 'mk_lm_tower_d1_tok_ids768_r4_e2d473'

def setup_inputs(seed: int=0):
    np.random.seed(seed)
    _w = jnp.asarray

    def _rec_inputs():
        import jax
        import jax.numpy as jnp
        _rk = jax.random.key(seed)
        x = jax.random.randint(jax.random.fold_in(_rk, 1), (16, 256), 0, 8000, jnp.int32)
        return x
    x = _rec_inputs()

    def _L0_tok_setup():
        import jax, jax.numpy as jnp
        import numpy as np
        V, S, D, H = (8000, 256, 192, 768)
        EPS = 1e-05

        def pos_encoding(seq_len, dim, dtype=jnp.float32):
            pos = jnp.arange(seq_len, dtype=dtype)[:, None]
            i = jnp.arange(dim, dtype=dtype)[None, :]
            ang = pos / jnp.power(jnp.asarray(10000.0, dtype), i / dim)
            even = (jnp.arange(dim) % 2 == 0)[None, :]
            return jnp.where(even, jnp.sin(ang), jnp.cos(ang))

        def layernorm2d(x, w, b):
            m = jnp.mean(x, axis=(-2, -1), keepdims=True)
            v = jnp.mean((x - m) ** 2, axis=(-2, -1), keepdims=True)
            return (x - m) / jnp.sqrt(v + EPS) * w + b
        key = jax.random.key(seed)
        ks = jax.random.split(key, 16)
        sc = 0.02
        emb = jax.random.normal(ks[0], (V, D), jnp.float32) * sc
        emb = emb.at[0].set(0.0)
        inp = {'x': jax.random.randint(ks[1], (8, S), 0, V), 'emb': emb, 'Wq': jax.random.normal(ks[2], (D, H), jnp.float32) * sc, 'bq': jnp.zeros((H,), jnp.float32), 'Wk': jax.random.normal(ks[3], (D, H), jnp.float32) * sc, 'bk': jnp.zeros((H,), jnp.float32), 'Wv': jax.random.normal(ks[4], (D, H), jnp.float32) * sc, 'bv': jnp.zeros((H,), jnp.float32), 'Wo': jax.random.normal(ks[5], (H, D), jnp.float32) * sc, 'bo': jnp.zeros((D,), jnp.float32), 'W1': jax.random.normal(ks[6], (D, H), jnp.float32) * sc, 'b1': jnp.zeros((H,), jnp.float32), 'W2': jax.random.normal(ks[7], (H, D), jnp.float32) * sc, 'b2': jnp.zeros((D,), jnp.float32), 'ln1_w': jnp.ones((S, D), jnp.float32), 'ln1_b': jnp.zeros((S, D), jnp.float32), 'ln2_w': jnp.ones((S, D), jnp.float32), 'ln2_b': jnp.zeros((S, D), jnp.float32)}
        return inp
    _L0_tok_all = _L0_tok_setup()
    _L0_tok_in = {k: v for k, v in _L0_tok_all.items() if k in ('emb', 'Wq', 'bq', 'Wk', 'bk', 'Wv', 'bv', 'Wo', 'bo', 'W1', 'b1', 'W2', 'b2', 'ln1_w', 'ln1_b', 'ln2_w', 'ln2_b')}
    del _L0_tok_all

    def _L0_attn_setup():
        import jax, jax.numpy as jnp
        import numpy as np
        LOOKBACK = 128
        TOPK = 16
        CHUNK = 32
        D = 192

        def _phrase_states(h, chunk):
            B, S, Dm = h.shape
            hc = h.reshape(B, S // chunk, chunk, Dm)
            pre = jnp.cumsum(hc, axis=2)
            denom = jnp.arange(1, chunk + 1, dtype=h.dtype).reshape(1, 1, chunk, 1)
            return (pre / denom).reshape(B, S, Dm)
        key = jax.random.key(seed)
        ks = jax.random.split(key, 11)
        std = 0.02
        inp = {'h': jax.random.normal(ks[0], (2, 512, D), jnp.float32)}
        names = ['Wq', 'Wk', 'Wv', 'Wpk', 'Wpv']
        for i, n in enumerate(names):
            inp[n] = jax.random.normal(ks[i + 1], (D, D), jnp.float32) * std
            inp['b' + n[1:]] = jax.random.normal(ks[i + 6], (D,), jnp.float32) * std
        return inp
    _L0_attn_all = _L0_attn_setup()
    _L0_attn_in = {k: v for k, v in _L0_attn_all.items() if k in ('Wq', 'bq', 'Wk', 'bk', 'Wv', 'bv', 'Wpk', 'bpk', 'Wpv', 'bpv')}
    del _L0_attn_all

    def _L0_ffn_setup():
        import jax, jax.numpy as jnp
        import numpy as np
        DIM = 192
        HEADS = 12
        EXPERTS = 8
        HID = 768
        TOP_K = 2
        LN_EPS = 1e-05

        def _layer_norm(x, g, b):
            mu = x.mean(-1, keepdims=True)
            var = ((x - mu) ** 2).mean(-1, keepdims=True)
            return (x - mu) * jax.lax.rsqrt(var + LN_EPS) * g + b

        def _attention(x, qkv_w, qkv_b, proj_w, proj_b):
            B, N, C = x.shape
            hd = C // HEADS
            qkv = (x @ qkv_w + qkv_b).reshape(B, N, 3, HEADS, hd).transpose(2, 0, 3, 1, 4)
            q, k, v = (qkv[0], qkv[1], qkv[2])
            attn = jax.nn.softmax(jnp.einsum('bhnd,bhmd->bhnm', q, k) * hd ** (-0.5), axis=-1)
            o = jnp.einsum('bhnm,bhmd->bhnd', attn, v).transpose(0, 2, 1, 3).reshape(B, N, C)
            return o @ proj_w + proj_b

        def _moe_mlp(xn, gate_w, w1, b1, w2, b2):
            T = xn.shape[0]
            logits = xn @ gate_w
            top_logits, top_idx = jax.lax.top_k(logits, TOP_K)
            top_gates = jax.nn.softmax(top_logits, axis=-1)
            gates = jnp.zeros((T, EXPERTS), xn.dtype).at[jnp.arange(T)[:, None], top_idx].set(top_gates)
            h = jax.nn.gelu(jnp.einsum('td,edh->teh', xn, w1) + b1, approximate=False)
            y = jnp.einsum('teh,ehd->ted', h, w2) + b2
            return jnp.einsum('ted,te->td', y, gates)
        key = jax.random.key(seed)
        ks = jax.random.split(key, 16)
        s = 0.02
        return {'x': jax.random.normal(ks[0], (8, 196, DIM), jnp.float32), 'ln1_g': jnp.ones((DIM,), jnp.float32), 'ln1_b': jnp.zeros((DIM,), jnp.float32), 'qkv_w': jax.random.normal(ks[1], (DIM, 3 * DIM), jnp.float32) * s, 'qkv_b': jnp.zeros((3 * DIM,), jnp.float32), 'proj_w': jax.random.normal(ks[2], (DIM, DIM), jnp.float32) * s, 'proj_b': jnp.zeros((DIM,), jnp.float32), 'ln2_g': jnp.ones((DIM,), jnp.float32), 'ln2_b': jnp.zeros((DIM,), jnp.float32), 'gate_w': jax.random.normal(ks[3], (DIM, EXPERTS), jnp.float32) * s, 'w1': jax.random.normal(ks[4], (EXPERTS, DIM, HID), jnp.float32) * s, 'b1': jnp.zeros((EXPERTS, HID), jnp.float32), 'w2': jax.random.normal(ks[5], (EXPERTS, HID, DIM), jnp.float32) * s, 'b2': jnp.zeros((EXPERTS, DIM), jnp.float32)}
    _L0_ffn_all = _L0_ffn_setup()
    _L0_ffn_in = {k: v for k, v in _L0_ffn_all.items() if k in ('ln1_g', 'ln1_b', 'qkv_w', 'qkv_b', 'proj_w', 'proj_b', 'ln2_g', 'ln2_b', 'gate_w', 'w1', 'b1', 'w2', 'b2')}
    del _L0_ffn_all
    return {'x': x, 'L0_tok_emb': _L0_tok_in['emb'], 'L0_tok_Wq': _L0_tok_in['Wq'], 'L0_tok_bq': _L0_tok_in['bq'], 'L0_tok_Wk': _L0_tok_in['Wk'], 'L0_tok_bk': _L0_tok_in['bk'], 'L0_tok_Wv': _L0_tok_in['Wv'], 'L0_tok_bv': _L0_tok_in['bv'], 'L0_tok_Wo': _L0_tok_in['Wo'], 'L0_tok_bo': _L0_tok_in['bo'], 'L0_tok_W1': _L0_tok_in['W1'], 'L0_tok_b1': _L0_tok_in['b1'], 'L0_tok_W2': _L0_tok_in['W2'], 'L0_tok_b2': _L0_tok_in['b2'], 'L0_tok_ln1_w': _L0_tok_in['ln1_w'], 'L0_tok_ln1_b': _L0_tok_in['ln1_b'], 'L0_tok_ln2_w': _L0_tok_in['ln2_w'], 'L0_tok_ln2_b': _L0_tok_in['ln2_b'], 'L0_attn_Wq': _L0_attn_in['Wq'], 'L0_attn_bq': _L0_attn_in['bq'], 'L0_attn_Wk': _L0_attn_in['Wk'], 'L0_attn_bk': _L0_attn_in['bk'], 'L0_attn_Wv': _L0_attn_in['Wv'], 'L0_attn_bv': _L0_attn_in['bv'], 'L0_attn_Wpk': _L0_attn_in['Wpk'], 'L0_attn_bpk': _L0_attn_in['bpk'], 'L0_attn_Wpv': _L0_attn_in['Wpv'], 'L0_attn_bpv': _L0_attn_in['bpv'], 'L0_ffn_ln1_g': _L0_ffn_in['ln1_g'], 'L0_ffn_ln1_b': _L0_ffn_in['ln1_b'], 'L0_ffn_qkv_w': _L0_ffn_in['qkv_w'], 'L0_ffn_qkv_b': _L0_ffn_in['qkv_b'], 'L0_ffn_proj_w': _L0_ffn_in['proj_w'], 'L0_ffn_proj_b': _L0_ffn_in['proj_b'], 'L0_ffn_ln2_g': _L0_ffn_in['ln2_g'], 'L0_ffn_ln2_b': _L0_ffn_in['ln2_b'], 'L0_ffn_gate_w': _L0_ffn_in['gate_w'], 'L0_ffn_w1': _L0_ffn_in['w1'], 'L0_ffn_b1': _L0_ffn_in['b1'], 'L0_ffn_w2': _L0_ffn_in['w2'], 'L0_ffn_b2': _L0_ffn_in['b2']}

def reference(x, L0_tok_emb, L0_tok_Wq, L0_tok_bq, L0_tok_Wk, L0_tok_bk, L0_tok_Wv, L0_tok_bv, L0_tok_Wo, L0_tok_bo, L0_tok_W1, L0_tok_b1, L0_tok_W2, L0_tok_b2, L0_tok_ln1_w, L0_tok_ln1_b, L0_tok_ln2_w, L0_tok_ln2_b, L0_attn_Wq, L0_attn_bq, L0_attn_Wk, L0_attn_bk, L0_attn_Wv, L0_attn_bv, L0_attn_Wpk, L0_attn_bpk, L0_attn_Wpv, L0_attn_bpv, L0_ffn_ln1_g, L0_ffn_ln1_b, L0_ffn_qkv_w, L0_ffn_qkv_b, L0_ffn_proj_w, L0_ffn_proj_b, L0_ffn_ln2_g, L0_ffn_ln2_b, L0_ffn_gate_w, L0_ffn_w1, L0_ffn_b1, L0_ffn_w2, L0_ffn_b2):
    import jax
    import jax.numpy as jnp

    def _L0_tok_ref(x, emb, Wq, bq, Wk, bk, Wv, bv, Wo, bo, W1, b1, W2, b2, ln1_w, ln1_b, ln2_w, ln2_b):
        import jax, jax.numpy as jnp
        import numpy as np
        V, S, D, H = (8000, 256, 192, 768)
        EPS = 1e-05

        def pos_encoding(seq_len, dim, dtype=jnp.float32):
            pos = jnp.arange(seq_len, dtype=dtype)[:, None]
            i = jnp.arange(dim, dtype=dtype)[None, :]
            ang = pos / jnp.power(jnp.asarray(10000.0, dtype), i / dim)
            even = (jnp.arange(dim) % 2 == 0)[None, :]
            return jnp.where(even, jnp.sin(ang), jnp.cos(ang))

        def layernorm2d(x, w, b):
            m = jnp.mean(x, axis=(-2, -1), keepdims=True)
            v = jnp.mean((x - m) ** 2, axis=(-2, -1), keepdims=True)
            return (x - m) / jnp.sqrt(v + EPS) * w + b
        y = emb[x]
        y = y + pos_encoding(y.shape[1], y.shape[2], y.dtype)
        q = y @ Wq + bq
        k = y @ Wk + bk
        v = y @ Wv + bv
        attn = jax.nn.softmax(jnp.einsum('bsh,bth->bst', q, k), axis=-1)
        a = jnp.einsum('bst,bth->bsh', attn, v) @ Wo + bo
        y = layernorm2d(y + a, ln1_w, ln1_b)
        f = jax.nn.gelu((y @ W1 + b1) @ W2 + b2, approximate=False)
        y = layernorm2d(y + f, ln2_w, ln2_b)
        return y

    def _L0_attn_ref(h, Wq, bq, Wk, bk, Wv, bv, Wpk, bpk, Wpv, bpv):
        import jax, jax.numpy as jnp
        import numpy as np
        LOOKBACK = 128
        TOPK = 16
        CHUNK = 32
        D = 192

        def _phrase_states(h, chunk):
            B, S, Dm = h.shape
            hc = h.reshape(B, S // chunk, chunk, Dm)
            pre = jnp.cumsum(hc, axis=2)
            denom = jnp.arange(1, chunk + 1, dtype=h.dtype).reshape(1, 1, chunk, 1)
            return (pre / denom).reshape(B, S, Dm)
        B, S, Dm = h.shape
        scale = 1.0 / np.sqrt(Dm).astype(np.float32)
        q = h @ Wq + bq
        k = h @ Wk + bk
        v = h @ Wv + bv
        ph = _phrase_states(h, CHUNK)
        pk = ph @ Wpk + bpk
        pv = ph @ Wpv + bpv
        k_prev = jnp.roll(k, 1, axis=1)
        v_prev = jnp.roll(v, 1, axis=1)
        pk_prev = jnp.roll(pk, 1, axis=1)
        pv_prev = jnp.roll(pv, 1, axis=1)
        seq_score = jnp.sum(q * k_prev, axis=-1, keepdims=True) * scale
        phr_score = jnp.sum(q * pk_prev, axis=-1, keepdims=True) * scale
        scores = jnp.einsum('btd,bsd->bts', q, k) * scale
        t_idx = jnp.arange(S)
        pos = t_idx[:, None] - LOOKBACK + jnp.arange(LOOKBACK)[None, :]
        valid = pos >= 0
        pos_c = jnp.clip(pos, 0, S - 1)
        band = jnp.take_along_axis(scores, pos_c[None], axis=2)
        band = jnp.where(valid[None], band, -jnp.inf)
        top_s, top_j = jax.lax.top_k(band, TOPK)
        top_pos = jnp.clip(t_idx[None, :, None] - LOOKBACK + top_j, 0, S - 1)
        sem_v = jax.vmap(lambda vb, pb: vb[pb])(v, top_pos)
        all_scores = jnp.concatenate([seq_score, top_s, phr_score], axis=-1)
        w = jax.nn.softmax(all_scores, axis=-1)
        vals = jnp.concatenate([v_prev[:, :, None], sem_v, pv_prev[:, :, None]], axis=2)
        summary = jnp.einsum('btn,btnd->btd', w, vals)
        mask = (t_idx > 0).astype(h.dtype)[None, :, None]
        return summary * mask

    def _L0_ffn_ref(x, ln1_g, ln1_b, qkv_w, qkv_b, proj_w, proj_b, ln2_g, ln2_b, gate_w, w1, b1, w2, b2):
        import jax, jax.numpy as jnp
        import numpy as np
        DIM = 192
        HEADS = 12
        EXPERTS = 8
        HID = 768
        TOP_K = 2
        LN_EPS = 1e-05

        def _layer_norm(x, g, b):
            mu = x.mean(-1, keepdims=True)
            var = ((x - mu) ** 2).mean(-1, keepdims=True)
            return (x - mu) * jax.lax.rsqrt(var + LN_EPS) * g + b

        def _attention(x, qkv_w, qkv_b, proj_w, proj_b):
            B, N, C = x.shape
            hd = C // HEADS
            qkv = (x @ qkv_w + qkv_b).reshape(B, N, 3, HEADS, hd).transpose(2, 0, 3, 1, 4)
            q, k, v = (qkv[0], qkv[1], qkv[2])
            attn = jax.nn.softmax(jnp.einsum('bhnd,bhmd->bhnm', q, k) * hd ** (-0.5), axis=-1)
            o = jnp.einsum('bhnm,bhmd->bhnd', attn, v).transpose(0, 2, 1, 3).reshape(B, N, C)
            return o @ proj_w + proj_b

        def _moe_mlp(xn, gate_w, w1, b1, w2, b2):
            T = xn.shape[0]
            logits = xn @ gate_w
            top_logits, top_idx = jax.lax.top_k(logits, TOP_K)
            top_gates = jax.nn.softmax(top_logits, axis=-1)
            gates = jnp.zeros((T, EXPERTS), xn.dtype).at[jnp.arange(T)[:, None], top_idx].set(top_gates)
            h = jax.nn.gelu(jnp.einsum('td,edh->teh', xn, w1) + b1, approximate=False)
            y = jnp.einsum('teh,ehd->ted', h, w2) + b2
            return jnp.einsum('ted,te->td', y, gates)
        B, N, C = x.shape
        x = x + _attention(_layer_norm(x, ln1_g, ln1_b), qkv_w, qkv_b, proj_w, proj_b)
        xn = _layer_norm(x, ln2_g, ln2_b).reshape(B * N, C)
        moe_out = _moe_mlp(xn, gate_w, w1, b1, w2, b2).reshape(B, N, C)
        return x + moe_out
    h = _L0_tok_ref(x, L0_tok_emb, L0_tok_Wq, L0_tok_bq, L0_tok_Wk, L0_tok_bk, L0_tok_Wv, L0_tok_bv, L0_tok_Wo, L0_tok_bo, L0_tok_W1, L0_tok_b1, L0_tok_W2, L0_tok_b2, L0_tok_ln1_w, L0_tok_ln1_b, L0_tok_ln2_w, L0_tok_ln2_b)
    h = h + _L0_attn_ref(_layernorm(h, axis=-1), L0_attn_Wq, L0_attn_bq, L0_attn_Wk, L0_attn_bk, L0_attn_Wv, L0_attn_bv, L0_attn_Wpk, L0_attn_bpk, L0_attn_Wpv, L0_attn_bpv)
    h = h + _L0_ffn_ref(_layernorm(h, axis=-1), L0_ffn_ln1_g, L0_ffn_ln1_b, L0_ffn_qkv_w, L0_ffn_qkv_b, L0_ffn_proj_w, L0_ffn_proj_b, L0_ffn_ln2_g, L0_ffn_ln2_b, L0_ffn_gate_w, L0_ffn_w1, L0_ffn_b1, L0_ffn_w2, L0_ffn_b2)
    return h

_drawn_inputs = setup_inputs


def setup_inputs(seed=0):
    import zlib

    import numpy as np

    out = dict(_drawn_inputs(seed))
    spreads = {'L0_tok_bq': (0.0, 0.8),
     'L0_tok_bk': (0.0, 2.0),
     'L0_tok_bv': (0.0, 0.1),
     'L0_tok_bo': (0.0, 0.1),
     'L0_tok_b1': (0.0, 0.279),
     'L0_tok_b2': (0.0, 0.1),
     'L0_tok_ln1_w': (1.0, 0.2),
     'L0_tok_ln1_b': (0.0, 0.1),
     'L0_tok_ln2_w': (1.0, 0.2),
     'L0_tok_ln2_b': (0.0, 0.1),
     'L0_ffn_ln1_g': (1.0, 0.6),
     'L0_ffn_ln1_b': (0.0, 0.8),
     'L0_ffn_qkv_b': (0.0, 0.446),
     'L0_ffn_proj_b': (0.0, 0.1),
     'L0_ffn_ln2_g': (1.0, 0.6),
     'L0_ffn_ln2_b': (0.0, 0.587),
     'L0_ffn_b1': (0.0, 0.747),
     'L0_ffn_b2': (0.0, 0.1)}
    factors = {'L0_tok_Wq': 2.682,
     'L0_attn_bq': 4.53,
     'L0_attn_bk': 64.0,
     'L0_attn_bv': 2.838,
     'L0_attn_Wpk': 8.0,
     'L0_attn_bpk': 64.0,
     'L0_attn_Wpv': 3.544,
     'L0_attn_bpv': 25.824}
    for name, (base, spread) in spreads.items():
        noise = np.random.default_rng([zlib.crc32(name.encode()), seed]).standard_normal(out[name].shape)
        drawn = base * np.exp(spread * noise) if base else spread * noise
        out[name] = jnp.asarray(drawn.astype(out[name].dtype))
    for name, factor in factors.items():
        out[name] = (out[name] * factor).astype(out[name].dtype)
    return out
```

```python
import concourse.bass as bass
from concourse import mybir
from contextlib import ExitStack

P = 128
B, S, D, H = 16, 256, 192, 768
V = 8000
C = 96
CK = (C, C + 1)
NT = S // P
HC = H // P
HEADS, HD = 12, 16
NJ = 3
NE = 8
CHUNK = 32
SLOTS = (0, 1)
ROUNDS = B // len(SLOTS)
STEP = 256
REG = B * S + STEP
MAX_STEPS = 2 * B * S // STEP + NE
MASKED = -1.0e30
TAKEN = -3.0e38
TAKEN_BELOW = -1.0e38
LN_EPS = 1e-5
CONSTS = {"ident": 128, "ones": 128, "mean": 128, "before": 128, "pos": 384, "mask": 384, "seq": 384,
          "phrase": 256, "real": 2, "expert": 8, "region": 8, "row": 1, "power": 4}

PE_STEPS = ["yT", "q1", "v1", "s1", "p1T", "a1", "stat1", "y1T", "f", "stat2",
            "hT", "ph", "q2", "q3", "v2", "pv", "phr", "s2", "wT", "sum",
            "xT", "qk0", "qk1", "qk2", "v3",
            "S0", "m0", "St0", "o0", "S1", "m1", "St1", "o1", "S2", "m2", "St2", "o2",
            "proj", "x2T", "logit", "rank"]
ACT_STEPS = ["yT", "v1", "p1", "y1T", "gelu", "hT", "v2", "pv", "e2", "wT",
             "xT", "qk1", "v3", "P0", "P1", "P2", "x2T", "eg"]
POOL_STEPS = ["idx", "r1", "r2", "r3", "r4", "r5", "base"]
DVE_STEPS = ["y", "q1", "max1", "p1T", "rr", "R1", "bs1", "mv1", "sq1", "st1", "nv1", "ve1", "z1", "y1",
             "R2", "bs2", "mv2", "sq2", "st2", "nv2", "ve2", "z2", "y2",
             "bs3", "mv3", "ve3", "h", "ph", "q2", "prod", "sc", "t1", "nm", "mr1", "t2", "mr2", "sel", "w",
             "den", "rden", "real", "u", "hn", "bs4", "mv4", "ve4", "x3", "qk0", "qk2",
             "max_0", "qm_0", "sh_0", "rc_0", "on_0", "max_1", "qm_1", "sh_1", "rc_1", "on_1",
             "max_2", "qm_2", "sh_2", "rc_2", "on_2",
             "xx", "bs5", "mv5", "ve5", "x2", "lg", "top", "ix", "ixf", "oh", "cnt", "dg",
             "pos", "run", "pick", "slotf", "slot", "slots", "g1a", "g1", "g2"]


class At:

    def __init__(self, names):
        self.names, self.next = names, {s: 0 for s in SLOTS}

    def step(self, s, name):
        assert self.names[self.next[s] % len(self.names)] == name, (name, self.names[self.next[s] % len(self.names)])
        self.next[s] += 1
        return 1

    def after(self, base, name):
        return base + (self.names.index(name) + 1)


def block_kernel(nc, A, out):
    f32, i32, u32 = mybir.dt.float32, mybir.dt.int32, mybir.dt.uint32
    ACT = mybir.ActivationFunctionType
    ALU = mybir.AluOpType
    AX = mybir.AxisListType
    ctx = ExitStack()
    with ctx:
        def sb(name, shape, dt=f32):
            return ctx.enter_context(nc.sbuf_tensor(name, shape, dt))

        def two(name, shape, dt=f32):
            return [sb(f"{name}_{s}", shape, dt) for s in SLOTS]

        def sem(name):
            return ctx.enter_context(nc.semaphore(name))

        const = sb("const", [P, sum(CONSTS.values())])
        K, at = {}, 0
        for name, width in CONSTS.items():
            K[name] = const[:, at:at + width]
            at += width
        ident = K["ident"]
        ids = sb("ids", [P, (B + 2) * NT], i32)
        arena = sb("arena", [P, HC * (4 * (D + 1) + 2 * D)])
        t_wq, t_wk, t_wv, t_w1 = (arena[:, i * HC * (D + 1):(i + 1) * HC * (D + 1)].rearrange("p (c n) -> p c n", c=HC)
                                  for i in range(4))
        t_wo, t_w2 = (arena[:, 4 * HC * (D + 1) + i * HC * D:4 * HC * (D + 1) + (i + 1) * HC * D].rearrange(
            "p (c n) -> p c n", c=HC) for i in range(2))
        e_sizes = (2 * H, HC * D, HC, D)
        e_at = [[h_ * sum(e_sizes) + sum(e_sizes[:i]) for i in range(5)] for h_ in range(2)]
        e_w1, e_w2, e_b1, e_b2 = ([arena[:, e_at[h_][i]:e_at[h_][i + 1]] for h_ in range(2)] for i in range(4))
        bo_row, b2_row = sb("bo_row", [C + 1, D]), sb("b2_row", [C + 1, D])
        a_wq, a_wk, a_wpk = (sb(f"a_{x}", [C, 2, D + 1]) for x in ("wq", "wk", "wpk"))
        m_qk1, m_qk2, m_qpk = (sb(f"m_{x}", [C + 1, 2, D + 1]) for x in ("qk1", "qk2", "qpk"))
        m_vo, m_ff = sb("m_vo", [C + 1, 2, D]), sb("m_ff", [C + 1, 2, D])
        w_v2, w_pv = sb("w_v2", [C + 1, 2, D]), sb("w_pv", [C + 1, 2, D])
        w_qk = sb("w_qk", [C + 1, 2, 2 * NJ * P])
        w_v3 = sb("w_v3", [C + 1, 2, D])
        w_proj = sb("w_proj", [P, NJ, D])
        w_gate = sb("w_gate", [C, 2, NE])
        ln1w, ln1b, ln2w, ln2b = (sb(f"ln{x}", [P, NT * D]) for x in ("1w", "1b", "2w", "2b"))
        affine = sb("affine", [C, 2, 4])
        base = sb("base", [P, B, NT * D])
        gates = sb("gates", [P, B, NT, 2])
        place = sb("place", [P, B, 2 * NT])
        place_t, place_s = sb("place_t", [P, B * 2 * NT]), sb("place_s", [P, B * 2 * NT])
        slot_of = sb("slot_of", [P, B, 2 * NT], u32)
        running = sb("running", [P, NE])
        emb = two("emb", [P, NT, D])
        idx = two("idx", [P, NT], i32)
        y, z, y2, h, hn, x3, x2, g_f = (two(x, [P, NT * D]) for x in ("y", "z", "y2", "h", "hn", "x3", "x2", "g_f"))
        xT = two("xT", [C + 1, 2, S])
        phT = two("phT", [C + 1, 2, S])
        qT = two("qT", [C + 1, 2, S])
        pr = two("pr", [C + 1, 2, S])
        vv, pv = two("vv", [P, NT, D]), two("pv", [P, NT, D])
        pP, pT = two("pP", [P, NT, S]), two("pT", [P, NT, S])
        sc, sr = two("sc", [P, 384]), two("sr", [P, 384])
        qk = two("qk", [P, NJ, 2, S])
        vx = two("vx", [P, NT, HEADS, 32])
        prob = two("prob", [P, 4, NT, S])
        mb = two("mb", [P, NT, P])
        sh = two("sh", [P, S])
        on = two("on", [P, NJ, S])
        sm = two("sm", [P, 96])
        top = two("top", [P, 2 * NT, 8])
        ix = two("ix", [P, NT, 8], u32)
        oh = two("oh", [P, 2, NT, NE])
        rk = two("rk", [P, 2, NT, NE])
        lg = two("lg", [P, NT, NE])
        cnt = two("cnt", [P, NT, NE])
        pos_e = two("pos_e", [P, NT, NE])
        slots = two("slots", [P, 2 * NT], u32)
        ps = [ctx.enter_context(nc.psum_tensor(f"ps{s}", [P, 4, 512], f32)) for s in SLOTS]
        dram_x = nc.dram_tensor("expert_rows", [NE * REG, D], f32, kind="Internal").ap()
        dram_y = nc.dram_tensor("expert_results", [MAX_STEPS * STEP, D], f32, kind="Internal").ap()
        zeros = sb("zeros", [P, D])
        pad = sb("pad", [P, 2 * NE], u32)
        table = sb("table", [P, 4 * NE])
        steps_of = sb("steps_of", [P, 2 * NE], i32)
        ex, eT, eh, ey = h[0], xT[0], prob[0], y[0]
        eh = prob[0][:].rearrange("p i t n -> p (i t) n")
        back = [prob[1][:].rearrange("p i t n -> p (i t n)")[:, s * 4 * D:(s + 1) * 4 * D].rearrange("p (k d) -> p k d", d=D)
                for s in SLOTS]
        final = z

        def small(s, at, n=1):
            return sm[s][:, at:at + n]

        loaded = sem("weights_loaded")
        consts_loaded = sem("consts_loaded")
        tower_loaded = sem("tower_loaded")
        fold_mm = sem("fold_products_in_psum")
        fold_cp = sem("fold_products_copied")
        pool_preset, dve_preset = sem("pool_preset"), sem("dve_preset")
        pe_done = [sem(f"pe_done_{s}") for s in SLOTS]
        act_done = [sem(f"act_done_{s}") for s in SLOTS]
        dve_done = [sem(f"dve_done_{s}") for s in SLOTS]
        pool_done = [sem(f"pool_done_{s}") for s in SLOTS]
        gathered = [sem(f"gathered_{s}") for s in SLOTS]
        scattered = [sem(f"scattered_{s}") for s in SLOTS]
        stored = sem("stored")
        dve_passed, pool_passed, pe_passed = sem("dve_passed"), sem("pool_passed"), sem("pe_passed")
        ranked, padded, padded_at = sem("counts_ready"), sem("padding_written"), sem("padding_places_ready")
        e_loaded = sem("expert_weights_loaded")
        x_loaded, x_turned, xT_ready = sem("x_loaded"), sem("x_turned"), sem("xT_ready")
        h_psum, h_ready, y_psum, y_ready = sem("h_psum"), sem("h_ready"), sem("y_psum"), sem("y_ready")
        y_stored, y_free = sem("y_stored"), sem("y_free")
        v_chain, y_zeroed, placed = sem("vector_chain"), sem("y_zeroed"), sem("result_places_ready")
        back_there = [sem(f"back_there_{s}") for s in SLOTS]
        back_free = [sem(f"back_free_{s}") for s in SLOTS]
        back_idx = sem("back_idx")
        summed = [sem(f"summed_{s}") for s in SLOTS]
        final_stored = [sem(f"final_stored_{s}") for s in SLOTS]
        final_free = [sem(f"final_free_{s}") for s in SLOTS]

        def each_step(eng, body, first=None):
            eng.wait_ge(ranked, 1)
            with eng.Fori(0, NE // 2) as pair:
                for par in range(2):
                    e = pair * 2 + par
                    count = eng.value_load(steps_of[0:1, bass.ds(e, 1)], min_val=1, max_val=B * S // STEP)
                    before = eng.value_load(steps_of[0:1, bass.ds(e + NE, 1)], min_val=0, max_val=MAX_STEPS - 1)
                    if first is not None:
                        first(par, e, before)
                    with eng.Fori(0, count) as t:
                        body(par, e, t, before + t)

        def total_steps(eng):
            return (eng.value_load(steps_of[0:1, NE - 1:NE], min_val=1, max_val=B * S // STEP)
                    + eng.value_load(steps_of[0:1, 2 * NE - 1:2 * NE], min_val=0, max_val=MAX_STEPS - 1))
        pe_at, act_at, dve_at, pool_at = At(PE_STEPS), At(ACT_STEPS), At(DVE_STEPS), At(POOL_STEPS)

        tower = [(t_wq, "t_wq"), (t_wk, "t_wk"), (t_wv, "t_wv"), (t_wo, "t_wo"), (t_w1, "t_w1"), (t_w2, "t_w2"),
                 (bo_row, "bo"), (b2_row, "b2"), (a_wq, "a_wq"), (a_wk, "a_wk"), (a_wpk, "a_wpk")]
        rest = [(w_v2, "w_v2"), (w_pv, "w_pv"), (w_qk, "w_qk"), (w_v3, "w_v3"), (w_proj, "w_proj"), (w_gate, "w_gate"),
                (ln1w, "ln1w"), (ln1b, "ln1b"), (ln2w, "ln2w"), (ln2b, "ln2b"), (affine, "affine")]
        block = ctx.enter_context(nc.Block())

        @block.sync
        def _(sp):
            sp.dma_start(ids[:], A["ids"]).then_inc(consts_loaded, 16)
            sp.dma_start(const[:], A["const"]).then_inc(consts_loaded, 16)
            for dst, name in tower:
                if name in ("bo", "b2"):
                    sp.dma_start(dst[C:C + 1, :], A[name]).then_inc(tower_loaded, 16)
                else:
                    sp.dma_start(dst[:], A[name]).then_inc(tower_loaded, 16)
            for dst, name in rest:
                if name.startswith("w_") and name not in ("w_proj", "w_gate"):
                    sp.dma_start(dst[0:C, 0, :], A[name][0:C, :]).then_inc(loaded, 16)
                    sp.dma_start(dst[:, 1, :], A[name][C:2 * C + 1, :]).then_inc(loaded, 16)
                else:
                    sp.dma_start(dst[:], A[name]).then_inc(loaded, 16)
            sp.wait_ge(pool_preset, 1)
            sp.dma_start(dram_y.rearrange("(p r) d -> p r d", p=P),
                         zeros[:].unsqueeze(1).to_broadcast([P, MAX_STEPS * STEP // P, D])).then_inc(y_zeroed, 16)
            for s in SLOTS:
                sp.wait_ge(scattered[s], 64 * ROUNDS)
            sp.wait_ge(padded, 16 * 2 * NE)

            def load_rows(par, e, t, g):
                sp.wait_ge(x_turned, g + 1)
                sp.dma_start(ex[:].rearrange("p (t d) -> p t d", d=D),
                             dram_x[bass.ds(e * REG + t * STEP, STEP), :].rearrange("(t p) d -> p t d", p=P)).then_inc(x_loaded, 16)

            each_step(sp, load_rows)
            sp.wait_ge(x_turned, total_steps(sp) + 1)
            sp.dma_start(ex[:].rearrange("p (t d) -> p t d", d=D),
                         dram_x[0:STEP, :].rearrange("(t p) d -> p t d", p=P)).then_inc(x_loaded, 16)
            with sp.Fori(0, ROUNDS) as n:
                for s in SLOTS:
                    sp.wait_ge(summed[s], n + 1)
                    sp.dma_start(out[bass.ds(n * 2 + s, 1), :, :].rearrange("b (t p) d -> p (b t) d", p=P),
                                 final[s][:].rearrange("p (t d) -> p t d", d=D)).then_inc(final_stored[s], 16)
                for s in SLOTS:
                    sp.wait_ge(final_stored[s], (n + 1) * 16)
                    sp.sem_inc(final_free[s], 1)
            for s in SLOTS:
                sp.wait_ge(final_stored[s], ROUNDS * 16)
                sp.wait_ge(gathered[s], 32 * (ROUNDS + 1))
            sp.wait_ge(e_loaded, 64 * (NE + 1))

        n_loaded = 16 * (len(rest) + 4)

        def products(lhsT, rhs, n_chunks, width):
            for half in range(2):
                for k in range(n_chunks):
                    last = nc.tensor.matmul(ps[0][0:C + 1, half, 0:width],
                                            lhsT[:, k, half * C:half * C + C + 1], rhs[:, k, 0:width],
                                            start=(k == 0), stop=(k == n_chunks - 1))
            return last

        folds = [(t_wq, t_wk, HC, D + 1, m_qk1, None), (t_wv, t_wo, HC, D, m_vo, bo_row), (t_w1, t_w2, HC, D, m_ff, b2_row),
                 (a_wq, a_wk, 2, D + 1, m_qk2, None), (a_wq, a_wpk, 2, D + 1, m_qpk, None)]

        @block.tensor
        def _(pe):
            pe.wait_ge(tower_loaded, 16 * len(tower))
            for k, (lhsT, rhs, n_chunks, width, _, _) in enumerate(folds):
                if k:
                    pe.wait_ge(fold_cp, k)
                products(lhsT, rhs, n_chunks, width).then_inc(fold_mm, 1)
            pe.wait_ge(fold_cp, len(folds))
            pe.wait_ge(loaded, n_loaded)
            pe.wait_ge(consts_loaded, 32)
            pe.wait_ge(pool_preset, 1 + len(SLOTS))
            pe.wait_ge(dve_preset, 3)

            def transposes(s, src, bank):
                v = src[s][:].rearrange("p (t d) -> p t d", d=D)
                for c in range(2):
                    for t in range(NT):
                        last = nc.tensor.transpose(ps[s][0:C, bank, c * S + t * P:c * S + (t + 1) * P],
                                                   v[:, t, c * C:(c + 1) * C], ident)
                return last

            def project_T(s, w, act, bank):
                for m in range(2):
                    for c in range(2):
                        last = nc.tensor.matmul(ps[s][0:C + 1, bank, m * S:(m + 1) * S],
                                                w[0:CK[c], c, m * C:m * C + C + 1], act[s][0:CK[c], c, :],
                                                start=(c == 0), stop=(c == 1))
                return last

            def project(s, w, act, bank, rows=CK, width=D):
                for t in range(NT):
                    for c in range(2):
                        last = nc.tensor.matmul(ps[s][:, bank, t * width:(t + 1) * width],
                                                act[s][0:rows[c], c, t * P:(t + 1) * P], w[0:rows[c], c, :],
                                                start=(c == 0), stop=(c == 1))
                return last

            with pe.Fori(0, ROUNDS) as n:
                vb, ab, gb = n * len(DVE_STEPS), n * len(ACT_STEPS), n * len(POOL_STEPS)

                def dve(s, name):
                    pe.wait_ge(dve_done[s], dve_at.after(vb, name))

                def act(s, name):
                    pe.wait_ge(act_done[s], act_at.after(ab, name))

                for s in SLOTS:
                    dve(s, "y")
                    transposes(s, y, 0).then_inc(pe_done[s], pe_at.step(s, "yT"))
                for s in SLOTS:
                    act(s, "yT")
                    project_T(s, m_qk1, xT, 1).then_inc(pe_done[s], pe_at.step(s, "q1"))
                    project(s, m_vo, xT, 2).then_inc(pe_done[s], pe_at.step(s, "v1"))
                for s in SLOTS:
                    dve(s, "q1")
                    for t in range(NT):
                        for c in range(2):
                            last = nc.tensor.matmul(ps[s][:, 3, t * S:(t + 1) * S], qT[s][0:CK[c], c, t * P:(t + 1) * P],
                                                    xT[s][0:CK[c], c, :], start=(c == 0), stop=(c == 1))
                    last.then_inc(pe_done[s], pe_at.step(s, "s1"))
                for s in SLOTS:
                    act(s, "p1")
                    for k in range(NT):
                        for t in range(NT):
                            last = nc.tensor.transpose(ps[s][:, 0, k * S + t * P:k * S + (t + 1) * P],
                                                       pP[s][:, t, k * P:(k + 1) * P], ident)
                    last.then_inc(pe_done[s], pe_at.step(s, "p1T"))
                for s in SLOTS:
                    dve(s, "p1T")
                    for t in range(NT):
                        for k in range(NT):
                            last = nc.tensor.matmul(ps[s][:, 1, t * D:(t + 1) * D], pT[s][:, k, t * P:(t + 1) * P],
                                                    vv[s][:, k, :], start=(k == 0), stop=(k == NT - 1))
                    last.then_inc(pe_done[s], pe_at.step(s, "a1"))
                for s in SLOTS:
                    dve(s, "sq1")
                    nc.tensor.matmul(ps[s][:, 2, 0:2], K["mean"], small(s, 8, 2), start=True,
                                     stop=True).then_inc(pe_done[s], pe_at.step(s, "stat1"))
                for s in SLOTS:
                    dve(s, "y1")
                    transposes(s, y, 0).then_inc(pe_done[s], pe_at.step(s, "y1T"))
                for s in SLOTS:
                    act(s, "y1T")
                    project(s, m_ff, xT, 3).then_inc(pe_done[s], pe_at.step(s, "f"))
                for s in SLOTS:
                    dve(s, "sq2")
                    nc.tensor.matmul(ps[s][:, 2, 0:2], K["mean"], small(s, 8, 2), start=True,
                                     stop=True).then_inc(pe_done[s], pe_at.step(s, "stat2"))
                for s in SLOTS:
                    dve(s, "h")
                    transposes(s, h, 0).then_inc(pe_done[s], pe_at.step(s, "hT"))
                    hv = h[s][:].rearrange("p (t d) -> p t d", d=D)
                    for c in range(2):
                        for t, lo, hi in ((0, 0, P + 1), (1, P + 1, S)):
                            last = nc.tensor.matmul(ps[s][0:C, 1, c * S + lo:c * S + hi], hv[:, t, c * C:(c + 1) * C],
                                                    K["phrase"][:, lo:hi], start=True, stop=True)
                    last.then_inc(pe_done[s], pe_at.step(s, "ph"))
                for s in SLOTS:
                    act(s, "hT")
                    project_T(s, m_qk2, xT, 2).then_inc(pe_done[s], pe_at.step(s, "q2"))
                    project_T(s, m_qpk, xT, 3).then_inc(pe_done[s], pe_at.step(s, "q3"))
                    project(s, w_v2, xT, 0).then_inc(pe_done[s], pe_at.step(s, "v2"))
                    dve(s, "ph")
                    project(s, w_pv, phT, 1).then_inc(pe_done[s], pe_at.step(s, "pv"))
                for s in SLOTS:
                    dve(s, "prod")
                    for t in range(NT):
                        for c in range(2):
                            last = nc.tensor.matmul(ps[s][:, 3, t:t + 1], pr[s][0:CK[c], c, t * P:(t + 1) * P],
                                                    K["ones"][0:CK[c], 0:1], start=(c == 0), stop=(c == 1))
                    last.then_inc(pe_done[s], pe_at.step(s, "phr"))
                    for t in range(NT):
                        for c in range(2):
                            last = nc.tensor.matmul(ps[s][:, 2, t * P:t * P + (t + 1) * P], qT[s][0:CK[c], c, t * P:(t + 1) * P],
                                                    xT[s][0:CK[c], c, 0:(t + 1) * P], start=(c == 0), stop=(c == 1))
                    last.then_inc(pe_done[s], pe_at.step(s, "s2"))
                for s in SLOTS:
                    dve(s, "w")
                    for k in range(3):
                        last = nc.tensor.transpose(ps[s][:, 3, k * P:(k + 1) * P], sc[s][:, k * P:(k + 1) * P], ident)
                    last.then_inc(pe_done[s], pe_at.step(s, "wT"))
                for s in SLOTS:
                    act(s, "wT")
                    nc.tensor.matmul(ps[s][:, 2, 0:D], sr[s][:, 0:P], vv[s][:, 0, :], start=True, stop=True)
                    for k in range(NT):
                        last = nc.tensor.matmul(ps[s][:, 2, D:2 * D], sr[s][:, (k + 1) * P:(k + 2) * P], vv[s][:, k, :],
                                                start=(k == 0), stop=(k == NT - 1))
                    last.then_inc(pe_done[s], pe_at.step(s, "sum"))
                for s in SLOTS:
                    dve(s, "x3")
                    transposes(s, h, 0).then_inc(pe_done[s], pe_at.step(s, "xT"))
                for s in SLOTS:
                    act(s, "xT")
                    for j in range(NJ):
                        for r in range(2):
                            for c in range(2):
                                last = nc.tensor.matmul(ps[s][:, 1 + j, r * S:(r + 1) * S],
                                                        w_qk[0:CK[c], c, (2 * j + r) * P:(2 * j + r + 1) * P],
                                                        xT[s][0:CK[c], c, :], start=(c == 0), stop=(c == 1))
                        last.then_inc(pe_done[s], pe_at.step(s, f"qk{j}"))
                    project(s, w_v3, xT, 0).then_inc(pe_done[s], pe_at.step(s, "v3"))
                for j in range(NJ):
                    for s in SLOTS:
                        if j == 0:
                            dve(s, "qk2")
                            act(s, "v3")
                        else:
                            dve(s, f"on_{j - 1}")
                        for t in range(NT):
                            for i in range(4):
                                q = slice(32 * i, 32 * i + 32)
                                last = nc.tensor.matmul(ps[s][:, i, t * S:(t + 1) * S], qk[s][q, j, 0, t * P:(t + 1) * P],
                                                        qk[s][q, j, 1, :], start=True, stop=True)
                        last.then_inc(pe_done[s], pe_at.step(s, f"S{j}"))
                    for s in SLOTS:
                        dve(s, f"max_{j}")
                        for t in range(NT):
                            last = nc.tensor.transpose(ps[s][:, 0, t * P:(t + 1) * P], mb[s][:, t, :], ident)
                        last.then_inc(pe_done[s], pe_at.step(s, f"m{j}"))
                    for s in SLOTS:
                        dve(s, f"qm_{j}")
                        for t in range(NT):
                            for i in range(4):
                                q = slice(32 * i, 32 * i + 32)
                                last = nc.tensor.matmul(ps[s][:, i, t * S:(t + 1) * S], qk[s][q, j, 1, t * P:(t + 1) * P],
                                                        qk[s][q, j, 0, :], start=True, stop=True)
                        last.then_inc(pe_done[s], pe_at.step(s, f"St{j}"))
                    for s in SLOTS:
                        act(s, f"P{j}")
                        for t in range(NT):
                            for i in range(4):
                                last = nc.tensor.matmul(ps[s][32 * i:32 * i + 32, 0, 0:S], vx[s][:, t, 4 * j + i, :],
                                                        prob[s][:, i, t, :], start=(t == 0), stop=(t == NT - 1))
                        last.then_inc(pe_done[s], pe_at.step(s, f"o{j}"))
                for s in SLOTS:
                    dve(s, "on_2")
                    for t in range(NT):
                        for j in range(NJ):
                            last = nc.tensor.matmul(ps[s][:, 1, t * D:(t + 1) * D], on[s][:, j, t * P:(t + 1) * P],
                                                    w_proj[:, j, :], start=(j == 0), stop=(j == NJ - 1))
                    last.then_inc(pe_done[s], pe_at.step(s, "proj"))
                for s in SLOTS:
                    dve(s, "x2")
                    transposes(s, x2, 0).then_inc(pe_done[s], pe_at.step(s, "x2T"))
                for s in SLOTS:
                    act(s, "x2T")
                    project(s, w_gate, xT, 2, rows=(C, C), width=NE).then_inc(pe_done[s], pe_at.step(s, "logit"))
                for s in SLOTS:
                    dve(s, "cnt")
                    r = ps[s][:, 3, 0:3 * NE]
                    nc.tensor.matmul(r[:, 0:NE], K["before"], cnt[s][:, 0, :], start=True, stop=True)
                    nc.tensor.matmul(r[:, NE:2 * NE], K["before"], cnt[s][:, 1, :], start=True, stop=False)
                    nc.tensor.matmul(r[:, NE:2 * NE], K["ones"], cnt[s][:, 0, :], start=False, stop=True)
                    nc.tensor.matmul(r[:, 2 * NE:3 * NE], K["ones"], cnt[s][:, 0, :], start=True, stop=False)
                    nc.tensor.matmul(r[:, 2 * NE:3 * NE], K["ones"], cnt[s][:, 1, :], start=False,
                                     stop=True).then_inc(pe_done[s], pe_at.step(s, "rank"))

            pe.sem_inc(x_turned, 1)
            rows = ex[:].rearrange("p (t d) -> p t d", d=D)

            def turn():
                for c in range(2):
                    for t in range(NT):
                        last = nc.tensor.transpose(ps[1][0:C, 2, c * S + t * P:c * S + (t + 1) * P],
                                                   rows[:, t, c * C:(c + 1) * C], ident)
                last.then_inc(x_turned, 1)

            pe.wait_ge(x_loaded, 16)
            turn()

            def weights(par, e, g):
                pe.wait_ge(e_loaded, e * 64 + 64)
                pe.sem_inc(pe_passed, 1)

            def step(par, e, t, g):
                def up(k):
                    w = e_w1[par][0:C, :].rearrange("p (c n) -> p c n", c=2)
                    for c in range(2):
                        last = nc.tensor.matmul(ps[0][:, k % 4, 0:STEP], w[:, c, k * P:(k + 1) * P], eT[0:C, c, :],
                                                start=(c == 0), stop=(c == 1))
                    last.then_inc(h_psum, 1)

                def down(k):
                    pe.wait_ge(h_ready, g * HC + (k + 1))
                    w = e_w2[par].rearrange("p (c n) -> p c n", c=HC)
                    for t_ in range(NT):
                        last = nc.tensor.matmul(ps[1][:, t_, 0:D], eh[:, k, t_ * P:(t_ + 1) * P], w[:, k, :],
                                                start=(k == 0), stop=(k == HC - 1))
                    return last

                pe.wait_ge(xT_ready, g + 1)
                up(0)
                for k in range(1, HC):
                    up(k)
                    if k == 1:
                        pe.wait_ge(y_ready, g + 1)
                    down(k - 1)
                pe.wait_ge(x_loaded, g * 16 + 32)
                turn()
                down(HC - 1).then_inc(y_psum, 1)

            each_step(pe, step, weights)

        @block.scalar
        def _(act):
            act.wait_ge(loaded, n_loaded)
            with act.Fori(0, ROUNDS) as n:
                pb, vb = n * len(PE_STEPS), n * len(DVE_STEPS)

                def pe(s, name):
                    act.wait_ge(pe_done[s], pe_at.after(pb, name))

                def dve(s, name):
                    act.wait_ge(dve_done[s], dve_at.after(vb, name))

                def copy_T(s, name):
                    pe(s, name)
                    nc.scalar.copy(xT[s][0:C, :, :], ps[s][0:C, 0, :]).then_inc(act_done[s], act_at.step(s, name))

                def affine_T(s, name, which):
                    pe(s, name)
                    for c in range(2):
                        last = nc.scalar.activation(xT[s][0:C, c, :], ps[s][0:C, 0, c * S:(c + 1) * S], ACT.Identity,
                                                    bias=affine[:, c, which + 1:which + 2], scale=affine[:, c, which:which + 1])
                    last.then_inc(act_done[s], act_at.step(s, name))

                for s in SLOTS:
                    copy_T(s, "yT")
                for s in SLOTS:
                    pe(s, "v1")
                    nc.scalar.copy(vv[s][:], ps[s][:, 2, 0:NT * D]).then_inc(act_done[s], act_at.step(s, "v1"))
                for s in SLOTS:
                    dve(s, "max1")
                    for t in range(NT):
                        last = nc.scalar.activation(pP[s][:, t, :], ps[s][:, 3, t * S:(t + 1) * S], ACT.Exp,
                                                    bias=small(s, t), accum_out=small(s, 2 + t))
                    last.then_inc(act_done[s], act_at.step(s, "p1"))
                for s in SLOTS:
                    copy_T(s, "y1T")
                for s in SLOTS:
                    pe(s, "f")
                    nc.scalar.activation(g_f[s][:], ps[s][:, 3, 0:NT * D], ACT.Gelu).then_inc(
                        act_done[s], act_at.step(s, "gelu"))
                for s in SLOTS:
                    copy_T(s, "hT")
                for s in SLOTS:
                    pe(s, "v2")
                    nc.scalar.copy(vv[s][:], ps[s][:, 0, 0:NT * D]).then_inc(act_done[s], act_at.step(s, "v2"))
                    pe(s, "pv")
                    nc.scalar.copy(pv[s][:], ps[s][:, 1, 0:NT * D]).then_inc(act_done[s], act_at.step(s, "pv"))
                for s in SLOTS:
                    dve(s, "nm")
                    nc.scalar.activation(pP[s][:, 0, 0:P], sc[s][:, 0:P], ACT.Exp, bias=small(s, 0))
                    nc.scalar.activation(pP[s][:, 1, :], sc[s][:, P:3 * P], ACT.Exp, bias=small(s, 1))
                    nc.scalar.activation(small(s, 6), small(s, 4), ACT.Exp, bias=small(s, 0))
                    nc.scalar.activation(small(s, 7), small(s, 5), ACT.Exp, bias=small(s, 1)).then_inc(
                        act_done[s], act_at.step(s, "e2"))
                for s in SLOTS:
                    pe(s, "wT")
                    nc.scalar.copy(sr[s][:], ps[s][:, 3, 0:3 * P]).then_inc(act_done[s], act_at.step(s, "wT"))
                for s in SLOTS:
                    affine_T(s, "xT", 0)
                for s in SLOTS:
                    pe(s, "qk1")
                    nc.scalar.copy(qk[s][:, 1, :, :], ps[s][:, 2, :]).then_inc(act_done[s], act_at.step(s, "qk1"))
                    pe(s, "v3")
                    nc.scalar.copy(vx[s][:, :, :, 0:HD],
                                   ps[s][:, 0, 0:NT * D].rearrange("p (t h d) -> p t h d", t=NT, h=HEADS)).then_inc(
                        act_done[s], act_at.step(s, "v3"))
                for j in range(NJ):
                    for s in SLOTS:
                        pe(s, f"St{j}")
                        nc.scalar.activation(prob[s][:].rearrange("p i t n -> p (i t n)"),
                                             ps[s][:].rearrange("p i n -> p (i n)"), ACT.Exp, scale=HD ** -0.5).then_inc(
                            act_done[s], act_at.step(s, f"P{j}"))
                for s in SLOTS:
                    affine_T(s, "x2T", 2)
                for s in SLOTS:
                    dve(s, "dg")
                    nc.scalar.activation(small(s, 46, 2), small(s, 44, 2), ACT.Exp).then_inc(
                        act_done[s], act_at.step(s, "eg"))

            def weights(par, e, g):
                act.wait_ge(e_loaded, e * 64 + 64)

            def step(par, e, t, g):
                for k in range(HC):
                    act.wait_ge(h_psum, g * HC + (k + 1))
                    nc.scalar.activation(eh[:, k, :], ps[0][:, k % 4, 0:STEP], ACT.Gelu,
                                         bias=e_b1[par][:, k:k + 1]).then_inc(h_ready, 1)

            each_step(act, step, weights)

        @block.gpsimd
        def _(pool):
            for s in SLOTS:
                nc.gpsimd.memset(vx[s][:], 1.0)
                last = nc.gpsimd.memset(mb[s][:], 0.0)
            last = nc.gpsimd.memset(zeros[:], 0.0)
            last.then_inc(pool_preset, 1)
            pool.wait_ge(consts_loaded, 32)

            def gather(s):
                for t in range(NT):
                    nc.gpsimd.indirect_dma_start(
                        out=emb[s][:, t, :], out_offset=None, in_=A["emb"],
                        in_offset=bass.IndirectOffsetOnAxis(ap=idx[s][:, t:t + 1].bitcast(u32), axis=0)).then_inc(gathered[s], 16)

            def load_expert(e, par):
                for dst, name in ((e_w1[par][0:C, :], "e_w1"), (e_w2[par], "e_w2"), (e_b1[par], "e_b1"), (e_b2[par], "e_b2")):
                    nc.gpsimd.dma_start(dst, A[name][bass.ds(e, 1), :, :].rearrange("e p n -> p (e n)")).then_inc(e_loaded, 16)

            pool.wait_ge(fold_cp, len(folds))
            for s in SLOTS:
                nc.gpsimd.tensor_copy(idx[s][:], ids[:, s * NT:(s + 1) * NT]).then_inc(pool_preset, 1)
                pool.wait_ge(pool_preset, 2 + s)
                gather(s)
            load_expert(0, 0)
            with pool.Fori(0, ROUNDS) as n:
                gb, vb, ab = n * len(POOL_STEPS), n * len(DVE_STEPS), n * len(ACT_STEPS)

                def dve(s, name):
                    pool.wait_ge(dve_done[s], dve_at.after(vb, name))

                def rsqrt(s, name, wait, at, width):
                    dve(s, wait)
                    nc.gpsimd.tensor_tensor(small(s, at + width, width), small(s, at, width), K["power"][:, 0:width],
                                            ALU.pow).then_inc(pool_done[s], pool_at.step(s, name))

                for s in SLOTS:
                    dve(s, "y")
                    nc.gpsimd.tensor_copy(idx[s][:], ids[:, bass.ds((n + 1) * (2 * NT) + s * NT, NT)]).then_inc(
                        pool_done[s], pool_at.step(s, "idx"))
                    pool.wait_ge(pool_done[s], pool_at.after(gb, "idx"))
                    pool.sem_inc(pool_passed, 1)
                    gather(s)
                for s in SLOTS:
                    rsqrt(s, "r1", "ve1", 14, 1)
                for s in SLOTS:
                    rsqrt(s, "r2", "ve2", 14, 1)
                for s in SLOTS:
                    rsqrt(s, "r3", "ve3", 20, 2)
                for s in SLOTS:
                    rsqrt(s, "r4", "ve4", 24, 4)
                for s in SLOTS:
                    rsqrt(s, "r5", "ve5", 20, 2)
                    nc.gpsimd.tensor_tensor(base[:, bass.ds(n * 2 + s, 1), :].rearrange("p b d -> p (b d)"), hn[s][:], x3[s][:],
                                            ALU.add).then_inc(pool_done[s], pool_at.step(s, "base"))
                for s in SLOTS:
                    dve(s, "slot")
                    pool.sem_inc(pool_passed, 1)
                    for k in range(2):
                        for t in range(NT):
                            nc.gpsimd.indirect_dma_start(
                                out=dram_x, out_offset=bass.IndirectOffsetOnAxis(ap=slots[s][:, k * NT + t:k * NT + t + 1], axis=0),
                                in_=x2[s][:, t * D:(t + 1) * D], in_offset=None).then_inc(scattered[s], 16)
                for s in SLOTS:
                    pool.wait_ge(scattered[s], (n + 1) * 64)
                    pool.sem_inc(pool_passed, 1)

            pool.wait_ge(y_zeroed, 16)
            pool.wait_ge(padded_at, 1)
            for k in range(2 * NE):
                nc.gpsimd.indirect_dma_start(out=dram_x, out_offset=bass.IndirectOffsetOnAxis(ap=pad[:, k:k + 1], axis=0),
                                             in_=zeros[:], in_offset=None).then_inc(padded, 16)
            pool.sem_inc(y_free, 1)

            def next_weights(par, e, g):
                pool.wait_ge(y_psum, g + 1)
                pool.sem_inc(pool_passed, 1)
                load_expert((e + 1) % NE, 1 - par)

            def store(par, e, t, g):
                pool.wait_ge(y_ready, g + 2)
                pool.sem_inc(pool_passed, 1)
                row = nc.s_assert_within(g, 0, MAX_STEPS - 1, skip_runtime_bounds_check_because=(
                    "the experts' steps sum to MAX_STEPS at most: two rows for each token and a part of a step for each expert"))
                nc.gpsimd.dma_start(dram_y[bass.ds(row * STEP, STEP), :].rearrange("(t p) d -> p t d", p=P),
                                    ey[:].rearrange("p (t d) -> p t d", d=D)).then_inc(y_stored, 16)
                pool.wait_ge(y_stored, g * 16 + 16)
                pool.sem_inc(y_free, 1)

            each_step(pool, store, next_weights)
            pool.wait_ge(placed, 1)
            with pool.Fori(0, ROUNDS) as n:
                for s in SLOTS:
                    pool.wait_ge(back_free[s], n + 1)
                    nc.gpsimd.tensor_copy(slots[s][:], slot_of[:, bass.ds(n * 2 + s, 1), :].rearrange("p b k -> p (b k)")).then_inc(
                        back_idx, 1)
                    pool.wait_ge(back_idx, n * 2 + s + 1)
                    pool.sem_inc(pool_passed, 1)
                    for k in range(2 * NT):
                        nc.gpsimd.indirect_dma_start(out=back[s][:, k, :], out_offset=None, in_=dram_y,
                                                     in_offset=bass.IndirectOffsetOnAxis(ap=slots[s][:, k:k + 1], axis=0)).then_inc(
                            back_there[s], 16)

        @block.vector
        def _(dve):
            for s in SLOTS:
                nc.vector.memset(xT[s][C:C + 1, :, :], 1.0)
                nc.vector.memset(phT[s][C:C + 1, :, :], 1.0)
                nc.vector.memset(small(s, 94), 0.0)
            dve.wait_ge(consts_loaded, 32)
            nc.vector.tensor_copy(running[:], K["region"]).then_inc(dve_preset, 1)
            for k, (_, _, _, width, dst, bias) in enumerate(folds):
                dve.wait_ge(fold_mm, k + 1)
                scale = float(D) ** -0.5 if k >= 3 else 1.0
                last = nc.vector.tensor_scalar(dst[:, :, 0:width], ps[0][0:C + 1, 0:2, 0:width], scale, None, ALU.mult)
                last.then_inc(fold_cp, 1)
                if bias is not None:
                    dve.wait_ge(fold_cp, k + 1)
                    nc.vector.tensor_tensor(dst[C:C + 1, 1, :], dst[C:C + 1, 1, :], bias[C:C + 1, :], ALU.add).then_inc(dve_preset, 1)
            dve.wait_ge(dve_preset, 3)
            dve.wait_ge(pool_preset, 1 + len(SLOTS))
            dve.wait_ge(loaded, n_loaded)
            with dve.Fori(0, ROUNDS) as n:
                pb, vb, ab, gb = (n * len(x) for x in (PE_STEPS, DVE_STEPS, ACT_STEPS, POOL_STEPS))

                def pe(s, name):
                    dve.wait_ge(pe_done[s], pe_at.after(pb, name))

                def act(s, name):
                    dve.wait_ge(act_done[s], act_at.after(ab, name))

                def pool(s, name):
                    dve.wait_ge(pool_done[s], pool_at.after(gb, name))

                def mark(ins, s, name):
                    ins.then_inc(dve_done[s], dve_at.step(s, name))

                def link(ins, s, name):
                    mark(ins, s, name)
                    dve.wait_ge(dve_done[s], dve_at.after(vb, name))

                def plain():
                    dve.sem_inc(dve_passed, 1)

                def tile(x, s, t):
                    return x[s][:, t * D:(t + 1) * D]

                def sums2d(s, k):
                    link(nc.vector.bn_stats(small(s, 32, 6), z[s][:]), s, f"bs{k}")
                    mv = small(s, 8, 2)
                    plain()
                    link(nc.vector.bn_aggr(mv, small(s, 32, 6)), s, f"mv{k}")
                    mark(nc.vector.scalar_tensor_tensor(mv[:, 1:2], mv[:, 0:1], mv[:, 0:1], mv[:, 1:2], ALU.mult, ALU.add),
                         s, f"sq{k}")

                def norm2d(s, k, w):
                    pe(s, f"stat{k}")
                    link(nc.vector.tensor_copy(small(s, 10, 2), ps[s][:, 2, 0:2]), s, f"st{k}")
                    link(nc.vector.scalar_tensor_tensor(small(s, 12), small(s, 10), small(s, 10), small(s, 11),
                                                        ALU.mult, ALU.subtract), s, f"nv{k}")
                    mark(nc.vector.tensor_scalar(small(s, 14), small(s, 12), -1.0, LN_EPS, ALU.mult, ALU.add), s, f"ve{k}")
                    mark(nc.vector.scalar_tensor_tensor(z[s][:], z[s][:], small(s, 10), w[:], ALU.subtract, ALU.mult),
                         s, f"z{k}")

                def norm2d_out(s, k, b, dst):
                    pool(s, f"r{k}")
                    dve.wait_ge(dve_done[s], dve_at.after(vb, f"z{k}"))
                    link(nc.vector.scalar_tensor_tensor(dst[s][:], z[s][:], small(s, 15), b[:], ALU.mult, ALU.add),
                         s, f"y{k}")

                def row_stats(s, k, src):
                    for t in range(NT):
                        last = nc.vector.bn_stats(small(s, 32 + 6 * t, 6), tile(src, s, t))
                    link(last, s, f"bs{k}")
                    plain()
                    for t in range(NT):
                        last = nc.vector.bn_aggr(small(s, 16 + 2 * t, 2), small(s, 32 + 6 * t, 6))
                    link(last, s, f"mv{k}")

                def variances(s):
                    return sm[s][:, 16:20].rearrange("p (t x) -> p t x", x=2)[:, :, 1]

                def standardise(dst, src, s, r):
                    for t in range(NT):
                        last = nc.vector.tensor_scalar(tile(dst, s, t), tile(src, s, t), small(s, 16 + 2 * t), small(s, r + t),
                                                       ALU.subtract, ALU.mult)
                    return last

                def bands(x, s):
                    return (x[s][:, 0:P], x[s][:, P:3 * P])

                for s in SLOTS:
                    dve.wait_ge(gathered[s], (n + 1) * 32)
                    mark(nc.vector.tensor_tensor(y[s][:], emb[s][:].rearrange("p t d -> p (t d)"), K["pos"], ALU.add), s, "y")
                for s in SLOTS:
                    pe(s, "q1")
                    mark(nc.vector.tensor_copy(flat(qT[s]), ps[s][0:C + 1, 1, :]), s, "q1")
                for s in SLOTS:
                    pe(s, "s1")
                    mark(nc.vector.tensor_reduce(small(s, 0, 2), ps[s][:, 3, :].rearrange("p (t n) -> p t n", t=NT),
                                                 AX.X, ALU.max, negate=True), s, "max1")
                for s in SLOTS:
                    pe(s, "p1T")
                    mark(nc.vector.tensor_copy(flat(pT[s]), ps[s][:, 0, :]), s, "p1T")
                    act(s, "p1")
                    link(nc.vector.reciprocal(small(s, 4, 2), small(s, 2, 2)), s, "rr")
                for s in SLOTS:
                    pe(s, "a1")
                    for t in range(NT):
                        last = nc.vector.scalar_tensor_tensor(tile(z, s, t), ps[s][:, 1, t * D:(t + 1) * D], small(s, 4 + t),
                                                              tile(y, s, t), ALU.mult, ALU.add)
                    link(last, s, "R1")
                    sums2d(s, 1)
                for s in SLOTS:
                    norm2d(s, 1, ln1w)
                for s in SLOTS:
                    norm2d_out(s, 1, ln1b, y)
                for s in SLOTS:
                    act(s, "gelu")
                    link(nc.vector.tensor_tensor(z[s][:], y[s][:], g_f[s][:], ALU.add), s, "R2")
                    sums2d(s, 2)
                for s in SLOTS:
                    norm2d(s, 2, ln2w)
                for s in SLOTS:
                    norm2d_out(s, 2, ln2b, y2)
                    row_stats(s, 3, y2)
                    mark(nc.vector.tensor_scalar(small(s, 20, 2), variances(s), LN_EPS, None, ALU.add), s, "ve3")
                for s in SLOTS:
                    pool(s, "r3")
                    mark(standardise(h, y2, s, 22), s, "h")
                for s in SLOTS:
                    pe(s, "ph")
                    mark(nc.vector.tensor_copy(phT[s][0:C, :, :].rearrange("p c n -> p (c n)"), ps[s][0:C, 1, :]), s, "ph")
                for s in SLOTS:
                    pe(s, "q2")
                    mark(nc.vector.tensor_copy(flat(qT[s]), ps[s][0:C + 1, 2, :]), s, "q2")
                    pe(s, "q3")
                    dve.wait_ge(dve_done[s], dve_at.after(vb, "ph"))
                    mark(nc.vector.tensor_tensor(flat(pr[s]), ps[s][0:C + 1, 3, :], flat(phT[s]), ALU.mult), s, "prod")
                for s in SLOTS:
                    pe(s, "s2")
                    nc.vector.tensor_copy(small(s, 4, 2), ps[s][:, 3, 0:NT])
                    link(nc.vector.tensor_tensor(sc[s][:], ps[s][:, 2, 0:3 * P], K["mask"], ALU.add), s, "sc")
                    plain()
                    for t in range(NT):
                        last = nc.vector.max(top[s][:, t, :], bands(sc, s)[t])
                    link(last, s, "t1")
                    for t in range(NT):
                        last = nc.vector.tensor_scalar(small(s, t), top[s][:, t, 0:1], small(s, 4 + t), -1.0, ALU.max, ALU.mult)
                    mark(last, s, "nm")
                    plain()
                    for t in range(NT):
                        last = nc.vector.match_replace(bands(sr, s)[t], top[s][:, t, :], bands(sc, s)[t], TAKEN)
                    link(last, s, "mr1")
                    plain()
                    for t in range(NT):
                        last = nc.vector.max(top[s][:, NT + t, :], bands(sr, s)[t])
                    link(last, s, "t2")
                    plain()
                    for t in range(NT):
                        last = nc.vector.match_replace(bands(sr, s)[t], top[s][:, NT + t, :], bands(sr, s)[t], TAKEN)
                    link(last, s, "mr2")
                    link(nc.vector.scalar_tensor_tensor(sr[s][:], sr[s][:], TAKEN_BELOW, K["seq"], ALU.is_lt, ALU.add), s, "sel")
                for s in SLOTS:
                    act(s, "e2")
                    e = (pP[s][:, 0, 0:P], pP[s][:, 1, :])
                    for t in range(NT):
                        last = nc.vector.scalar_tensor_tensor(bands(sc, s)[t], e[t], 1.0, bands(sr, s)[t], ALU.mult, ALU.mult,
                                                              accum_out=small(s, 52 + t))
                    link(last, s, "w")
                    link(nc.vector.tensor_tensor(small(s, 52, 2), small(s, 52, 2), small(s, 6, 2), ALU.add), s, "den")
                    link(nc.vector.reciprocal(small(s, 54, 2), small(s, 52, 2)), s, "rden")
                    link(nc.vector.tensor_tensor(small(s, 54, 2), small(s, 54, 2), K["real"], ALU.mult), s, "real")
                for s in SLOTS:
                    pe(s, "sum")
                    for t in range(NT):
                        last = nc.vector.scalar_tensor_tensor(tile(h, s, t), pv[s][:, t, :], small(s, 6 + t),
                                                              ps[s][:, 2, t * D:(t + 1) * D], ALU.mult, ALU.add)
                    link(last, s, "u")
                    for t in range(NT):
                        last = nc.vector.scalar_tensor_tensor(tile(hn, s, t), tile(h, s, t), small(s, 54 + t), tile(y2, s, t),
                                                              ALU.mult, ALU.add)
                    link(last, s, "hn")
                    row_stats(s, 4, hn)
                    nc.vector.tensor_scalar(small(s, 24, 2), variances(s), LN_EPS, None, ALU.add)
                    mark(nc.vector.tensor_scalar(small(s, 26, 2), variances(s), 1.0 + LN_EPS, LN_EPS * LN_EPS, ALU.mult, ALU.add),
                         s, "ve4")
                for s in SLOTS:
                    pool(s, "r4")
                    standardise(h, hn, s, 30)
                    mark(standardise(x3, hn, s, 28), s, "x3")
                for s in SLOTS:
                    pe(s, "qk0")
                    mark(nc.vector.tensor_copy(qk[s][:, 0, :, :].rearrange("p r n -> p (r n)"), ps[s][:, 1, :]), s, "qk0")
                    pe(s, "qk2")
                    mark(nc.vector.tensor_copy(qk[s][:, 2, :, :].rearrange("p r n -> p (r n)"), ps[s][:, 3, :]), s, "qk2")
                for j in range(NJ):
                    for s in SLOTS:
                        pe(s, f"S{j}")
                        mark(nc.vector.tensor_reduce(mb[s][:].rearrange("p t (i x) -> p t i x", x=32)[:, :, :, HD],
                                                     ps[s][:].rearrange("p i (t n) -> p t i n", t=NT), AX.X, ALU.max), s, f"max_{j}")
                    for s in SLOTS:
                        pe(s, f"m{j}")
                        q = qk[s][:, j, 0, :]
                        mark(nc.vector.tensor_tensor(q, ps[s][:, 0, 0:S], q, ALU.add), s, f"qm_{j}")
                    for s in SLOTS:
                        pe(s, f"o{j}")
                        plain()
                        link(nc.vector.stream_shuffle(sh[s][:], ps[s][:, 0, 0:S], [HD + i % HD for i in range(32)]), s, f"sh_{j}")
                        link(nc.vector.reciprocal(sh[s][:], sh[s][:]), s, f"rc_{j}")
                        mark(nc.vector.tensor_tensor(on[s][:, j, :], ps[s][:, 0, 0:S], sh[s][:], ALU.mult), s, f"on_{j}")
                for s in SLOTS:
                    pe(s, "proj")
                    link(nc.vector.tensor_tensor(x3[s][:], ps[s][:, 1, 0:NT * D], x3[s][:], ALU.add), s, "xx")
                    row_stats(s, 5, x3)
                    mark(nc.vector.tensor_scalar(small(s, 20, 2), variances(s), LN_EPS, None, ALU.add), s, "ve5")
                for s in SLOTS:
                    pool(s, "r5")
                    mark(standardise(x2, x3, s, 22), s, "x2")
                for s in SLOTS:
                    pe(s, "logit")
                    link(nc.vector.tensor_copy(flat(lg[s]), ps[s][:, 2, 0:NT * NE]), s, "lg")
                    plain()
                    for t in range(NT):
                        last = nc.vector.max(top[s][:, t, :], lg[s][:, t, :])
                    link(last, s, "top")
                    plain()
                    for t in range(NT):
                        last = nc.vector.max_index(ix[s][:, t, :], top[s][:, t, :], lg[s][:, t, :])
                    link(last, s, "ix")
                    chosen = small(s, 56, 4).rearrange("p (k t) -> p k t", k=2)
                    link(nc.vector.tensor_copy(chosen, ix[s][:, :, 0:2].rearrange("p t k -> p k t")), s, "ixf")
                    for k in range(2):
                        last = nc.vector.tensor_tensor(oh[s][:, k, :, :], K["expert"].unsqueeze(1).to_broadcast([P, NT, NE]),
                                                       chosen[:, k, :].unsqueeze(2).to_broadcast([P, NT, NE]), ALU.is_equal)
                    link(last, s, "oh")
                    mark(nc.vector.tensor_tensor(flat(cnt[s]), flat(oh[s][:, 0, :, :]), flat(oh[s][:, 1, :, :]), ALU.add), s, "cnt")
                    mark(nc.vector.tensor_tensor(small(s, 44, 2), top[s][:, 0:NT, 1], top[s][:, 0:NT, 0], ALU.subtract), s, "dg")
                for s in SLOTS:
                    pe(s, "rank")
                    link(nc.vector.tensor_tensor(pos_e[s][:], ps[s][:, 3, 0:NT * NE].rearrange("p (t e) -> p t e", t=NT),
                                                 running[:].unsqueeze(1).to_broadcast([P, NT, NE]), ALU.add), s, "pos")
                    link(nc.vector.tensor_tensor(running[:], ps[s][:, 3, NT * NE:3 * NE], running[:], ALU.add), s, "run")
                    link(nc.vector.tensor_tensor(rk[s][:], oh[s][:], pos_e[s][:].unsqueeze(1).to_broadcast([P, 2, NT, NE]),
                                                 ALU.mult), s, "pick")
                    link(nc.vector.tensor_reduce(small(s, 60, 4), rk[s][:].rearrange("p k t e -> p (k t) e"), AX.X, ALU.add),
                         s, "slotf")
                    link(nc.vector.tensor_copy(slots[s][:], small(s, 60, 4)), s, "slot")
                    mark(nc.vector.tensor_copy(place[:, bass.ds(n * 2 + s, 1), :].rearrange("p b k -> p (b k)"), small(s, 60, 4)),
                         s, "slots")
                    act(s, "eg")
                    link(nc.vector.tensor_scalar(small(s, 48, 2), small(s, 46, 2), 1.0, None, ALU.add), s, "g1a")
                    link(nc.vector.reciprocal(small(s, 50, 2), small(s, 48, 2)), s, "g1")
                    g = gates[:, bass.ds(n * 2 + s, 1), :, :].rearrange("p b t k -> p (b t) k")
                    nc.vector.tensor_copy(g[:, :, 0], small(s, 50, 2))
                    mark(nc.vector.tensor_tensor(g[:, :, 1], small(s, 46, 2), small(s, 50, 2), ALU.mult), s, "g2")

            v_links = [0]

            def link_v(ins):
                v_links[0] += 1
                ins.then_inc(v_chain, 1)
                dve.wait_ge(v_chain, v_links[0])

            for k in range(2):
                last = nc.vector.tensor_scalar(table[:, k * NE:(k + 1) * NE], running[:], K["row"], float(k * P), ALU.add, ALU.add)
            link_v(last)
            nc.vector.tensor_copy(pad[:], table[:, 0:2 * NE]).then_inc(padded_at, 1)
            link_v(nc.vector.tensor_tensor(table[:, 2 * NE:3 * NE], running[:], K["region"], ALU.subtract))
            link_v(nc.vector.tensor_scalar(table[:, 3 * NE:4 * NE], table[:, 2 * NE:3 * NE], 1.0, float(STEP - 1), ALU.max,
                                           ALU.add))
            link_v(nc.vector.tensor_copy(steps_of[:, NE:2 * NE], table[:, 3 * NE:4 * NE]))
            link_v(nc.vector.tensor_scalar(steps_of[:, 0:NE], steps_of[:, NE:2 * NE], STEP.bit_length() - 1, None,
                                           ALU.logical_shift_right))
            link_v(nc.vector.tensor_copy(table[:, 0:NE], steps_of[:, 0:NE]))
            link_v(nc.vector.tensor_tensor_scan(table[:, NE:2 * NE], K["ones"][:, 0:NE], table[:, 0:NE], 0.0, ALU.mult, ALU.add))
            link_v(nc.vector.tensor_tensor(table[:, 2 * NE:3 * NE], table[:, NE:2 * NE], table[:, 0:NE], ALU.subtract))
            nc.vector.tensor_copy(steps_of[:, NE:2 * NE], table[:, 2 * NE:3 * NE]).then_inc(ranked, 1)
            dve.sem_inc(y_ready, 1)

            def spread(g):
                dve.wait_ge(x_turned, g + 2)
                for c in range(2):
                    last = nc.vector.tensor_scalar(eT[0:C, c, :], ps[1][0:C, 2, c * S:(c + 1) * S], affine[:, c, 2:3],
                                                   affine[:, c, 3:4], ALU.mult, ALU.add)
                last.then_inc(xT_ready, 1)

            def weights(par, e, g):
                dve.wait_ge(e_loaded, e * 64 + 64)
                dve.sem_inc(dve_passed, 1)

            def step(par, e, t, g):
                spread(g + 1)
                dve.wait_ge(y_psum, g + 1)
                dve.wait_ge(y_free, g + 1)
                nc.vector.tensor_tensor(ey[:].rearrange("p (t d) -> p t d", d=D), ps[1][:, 0:2, 0:D],
                                        e_b2[par].unsqueeze(1).to_broadcast([P, NT, D]), ALU.add).then_inc(y_ready, 1)

            spread(0)
            shift, jump = table[:, 3 * NE:4 * NE], table[:, 0:NE]
            link_v(nc.vector.scalar_tensor_tensor(shift, table[:, 2 * NE:3 * NE], float(STEP), K["region"], ALU.mult,
                                                  ALU.subtract))
            link_v(nc.vector.tensor_tensor(jump[:, 1:NE], shift[:, 1:NE], shift[:, 0:NE - 1], ALU.subtract))
            flat_place = place[:].rearrange("p b k -> p (b k)")
            link_v(nc.vector.tensor_copy(place_s[:], flat_place))
            for e in range(1, NE):
                link_v(nc.vector.tensor_scalar(place_t[:], flat_place, float(e * REG), jump[:, e:e + 1], ALU.is_ge, ALU.mult))
                link_v(nc.vector.tensor_tensor(place_s[:], place_s[:], place_t[:], ALU.add))
            nc.vector.tensor_copy(slot_of[:].rearrange("p b k -> p (b k)"), place_s[:]).then_inc(placed, 1)
            each_step(dve, step, weights)
            for s in SLOTS:
                dve.sem_inc(back_free[s], 1)
                dve.sem_inc(final_free[s], 1)
            with dve.Fori(0, ROUNDS) as n:
                for s in SLOTS:
                    b_ = n * 2 + s
                    dve.wait_ge(back_there[s], (n + 1) * (16 * 2 * NT))
                    for t in range(NT):
                        acc = base[:, bass.ds(b_, 1), t * D:(t + 1) * D].rearrange("p b d -> p (b d)")
                        g_ = gates[:, bass.ds(b_, 1), t, :].rearrange("p b k -> p (b k)")
                        last = nc.vector.scalar_tensor_tensor(acc, back[s][:, t, :], g_[:, 0:1], acc, ALU.mult, ALU.add)
                    last.then_inc(v_chain, 1)
                    dve.wait_ge(v_chain, n * 2 + (v_links[0] + 1 + s))
                    dve.wait_ge(final_free[s], n + 1)
                    for t in range(NT):
                        acc = base[:, bass.ds(b_, 1), t * D:(t + 1) * D].rearrange("p b d -> p (b d)")
                        g_ = gates[:, bass.ds(b_, 1), t, :].rearrange("p b k -> p (b k)")
                        last = nc.vector.scalar_tensor_tensor(final[s][:, t * D:(t + 1) * D], back[s][:, NT + t, :], g_[:, 1:2],
                                                              acc, ALU.mult, ALU.add)
                    last.then_inc(summed[s], 1)
                    dve.wait_ge(summed[s], n + 1)
                    dve.sem_inc(back_free[s], 1)


def flat(x):
    x = x[:] if not isinstance(x, bass.AP) else x
    return x.rearrange("p a b -> p (a b)")


def constants(np):
    p = np.arange(P)[:, None]
    f = np.float32
    c = {"ident": np.eye(P), "ones": np.ones((P, P)), "mean": np.full((P, P), 1.0 / P), "before": p < np.arange(P)[None, :]}
    pos = np.arange(S, dtype=f)[:, None]
    i = np.arange(D, dtype=f)[None, :]
    ang = pos / np.power(f(10000.0), i / f(D))
    enc = np.where(np.arange(D)[None, :] % 2 == 0, np.sin(ang), np.cos(ang)).astype(f)
    c["pos"] = enc.reshape(NT, P, D).transpose(1, 0, 2).reshape(P, NT * D)
    s = np.arange(2 * P)[None, :]
    c["mask"] = np.concatenate([np.where(s[:, :P] < p, 0.0, MASKED), np.where((s >= p) & (s < p + P), 0.0, MASKED)], 1)
    c["seq"] = np.concatenate([s[:, :P] == p - 1, s == p + P - 1], 1)
    ph = np.zeros((P, S))
    for t in range(1, S):
        first = (t - 1) // CHUNK * CHUNK
        own = 0 if t <= P else P
        ph[first - own:t - own, t] = 1.0 / (t - first)
    c["phrase"] = ph
    c["real"] = np.stack([np.arange(P) > 0, np.ones(P)], 1)
    c["expert"] = np.tile(np.arange(NE), (P, 1))
    c["region"] = np.tile(np.arange(NE) * REG, (P, 1))
    c["row"] = p
    c["power"] = np.full((P, 4), -0.5)
    return np.concatenate([c[name].astype(f) for name in CONSTS], 1)


def layouts(np, inp):
    g = {k: np.ascontiguousarray(v) for k, v in inp.items()}
    f = np.float32
    rows = lambda w, b: np.concatenate([w, b[None, :]], 0)
    hid = lambda w: w.reshape(HC, P, -1).transpose(1, 0, 2)
    a = {"const": constants(np)}
    ids = np.zeros(((B + 2) * NT, P), np.int32)
    ids[:B * NT] = g["x"].reshape(B * NT, P)
    a["ids"] = ids.T
    a["emb"] = g["L0_tok_emb"]
    t, n, m = "L0_tok_", "L0_attn_", "L0_ffn_"
    a["t_wq"], a["t_wk"], a["t_wv"], a["t_w1"] = (hid(rows(g[t + w], g[t + b]).T) for w, b in
                                                 (("Wq", "bq"), ("Wk", "bk"), ("Wv", "bv"), ("W1", "b1")))
    a["t_wo"], a["t_w2"] = hid(g[t + "Wo"]), hid(g[t + "W2"])
    a["bo"], a["b2"] = g[t + "bo"][None, :], g[t + "b2"][None, :]
    a["a_wq"], a["a_wk"], a["a_wpk"] = (rows(g[n + w], g[n + b]).T.reshape(2, C, D + 1).transpose(1, 0, 2) for w, b in
                                        (("Wq", "bq"), ("Wk", "bk"), ("Wpk", "bpk")))
    a["w_v2"], a["w_pv"] = rows(g[n + "Wv"], g[n + "bv"]), rows(g[n + "Wpv"], g[n + "bpv"])
    w = rows(g[m + "qkv_w"], g[m + "qkv_b"])
    qk = np.zeros((D + 1, NJ, 2, 4, 32), f)
    qk[..., :HD] = w[:, :2 * D].reshape(D + 1, 2, NJ, 4, HD).transpose(0, 2, 1, 3, 4)
    qk[D, :, 1, :, HD] = -1.0
    a["w_qk"] = qk.reshape(D + 1, -1)
    a["w_v3"] = w[:, 2 * D:]
    proj = np.zeros((4, 32, NJ, D), f)
    proj[:, :HD] = g[m + "proj_w"].reshape(NJ, 4, HD, D).transpose(1, 2, 0, 3)
    proj[0, HD, 0] = g[m + "proj_b"]
    a["w_proj"] = proj.reshape(P, NJ, D)
    a["w_gate"] = g[m + "gate_w"].reshape(2, C, NE).transpose(1, 0, 2)
    sd = lambda x: x.reshape(NT, P, D).transpose(1, 0, 2).reshape(P, NT * D)
    a["ln1w"], a["ln1b"], a["ln2w"], a["ln2b"] = (sd(g[t + x]) for x in ("ln1_w", "ln1_b", "ln2_w", "ln2_b"))
    a["affine"] = np.stack([g[m + x] for x in ("ln1_g", "ln1_b", "ln2_g", "ln2_b")], 1).reshape(2, C, 4).transpose(1, 0, 2)
    a["e_b1"] = g[m + "b1"].reshape(NE, HC, P).transpose(0, 2, 1)
    a["e_b2"] = np.broadcast_to(g[m + "b2"][:, None], (NE, P, D))
    a["e_w1"] = g[m + "w1"].reshape(NE, 2, C, H).transpose(0, 2, 1, 3).reshape(NE, C, 2 * H)
    a["e_w2"] = g[m + "w2"].reshape(NE, HC, P, D).transpose(0, 2, 1, 3).reshape(NE, P, HC * D)
    return {k: np.ascontiguousarray(v) for k, v in a.items()}


def kernel(**inputs):
    import numpy as np
    import concourse.bacc as bacc
    from concourse.bass_utils import run_bass_kernel_spmd as run

    nc = bacc.Bacc("TRN2", target_bir_lowering=False, num_devices=1)
    arrays = layouts(np, {k: np.asarray(v) for k, v in inputs.items()})
    A = {k: nc.dram_tensor(f"in_{k}", v.shape, mybir.dt.from_np(v.dtype), kind="ExternalInput").ap() for k, v in arrays.items()}
    out = nc.dram_tensor("result", (B, S, D), mybir.dt.float32, kind="ExternalOutput").ap()
    block_kernel(nc, A, out)
    r = run(nc, [{f"in_{k}": v for k, v in arrays.items()}], core_ids=[0])
    return r.results[0]["result"]
```

```python
import concourse.bass as bass
from concourse import mybir
from contextlib import ExitStack

P = 128
B, S, D, H = 16, 256, 192, 768
C = 96
CK = (C, C + 1)
NT = S // P
HC = H // P
HEADS, HD = 12, 16
NJ = 3
NE = 8
CHUNK = 32
SLOTS = (0, 1)
ROUNDS = B // len(SLOTS)
STEP = 256
REG = STEP + B * S
ROW = D + 2
RESULTS = 2 * B * S
MAX_STEPS = 2 * B * S // STEP + NE
QK_BANK = (2, 0, 1)
BACK = 8
MASKED = -1.0e30
TAKEN = -3.0e38
TAKEN_BELOW = -1.0e38
LN_EPS = 1e-5
CONSTS = {"ident": 128, "ones": 128, "mean": 128, "before": 128, "pos": 384, "mask": 384, "seq": 384,
          "phrase": 256, "real": 2, "head": 4, "expert": 8, "region": 8, "place": B * NT, "idle": NT, "power": 4}

PE_STEPS = ["yT", "q1", "v1", "s1", "p1T", "a1", "stat1", "y1T", "f", "stat2",
            "hT", "ph", "q2", "q3", "v2", "pv", "phr", "s2", "wT", "sum",
            "xT", "qk0", "v3", "qk1", "qk2",
            "S0b", "S0a", "m0", "E0b", "E0a", "S1b", "o0", "S1a", "m1", "E1b", "E1a", "S2b", "o1", "S2a", "m2", "E2b", "E2a",
            "o2", "proj", "x2T", "logit", "rank"]
ACT_STEPS = ["yT", "v1", "p1", "y1T", "gelu", "hT", "v2", "pv", "e2", "wT",
             "xT", "v3", "qk1", "P0b", "P0a", "oc0", "P1b", "P1a", "oc1", "P2b", "P2a", "oc2", "x2T"]
POOL_STEPS = ["idx", "r1", "r2", "r3", "r4", "r5", "base"]
DVE_STEPS = ["y", "q1", "max1", "p1T", "rr", "R1", "bs1", "mv1", "sq1", "st1", "nv1", "ve1", "z1", "y1",
             "R2", "bs2", "mv2", "sq2", "st2", "nv2", "ve2", "z2", "y2",
             "bs3", "mv3", "ve3", "h", "ph", "q2", "prod", "sc", "t1", "nm", "mr1", "t2", "mr2", "sel", "w",
             "den", "rden", "real", "u", "hn", "bs4", "mv4", "ve4", "x3", "qk0", "qk2",
             "max0b", "max0a", "qm0", "max1b", "sh0", "rc0", "on0", "max1a", "qm1",
             "max2b", "sh1", "rc1", "on1", "max2a", "qm2", "sh2", "rc2", "on2",
             "xx", "bs5", "mv5", "ve5", "x2", "lg", "top", "ix", "ixf", "oh", "cnt", "dg",
             "pos", "run", "pick", "slotf", "slot"]

STAGES = ["y", "yT", "q1", "v1", "s1", "p1T", "a1", "a1_stats", "stat1", "y1", "y1T", "f", "f_stats", "stat2",
          "y2", "y2_stats", "h", "h_ph", "q2", "q3", "v2", "pv", "s2", "s2_top", "topk1", "topk2", "select", "w",
          "sum", "sum_stats", "x3", "xT", "qk0", "v3", "qk1", "qk2", "S0b", "S0a", "m0", "E0b", "E0a", "S1b", "o0",
          "n0", "S1a", "m1", "E1b", "E1a", "S2b", "o1", "n1", "S2a", "m2", "E2b", "E2a", "o2", "n2", "proj",
          "proj_stats", "x2", "x2T", "logit", "chosen", "rank", "place"]
TURNS = ["y.0", "E0a.1", "yT.0", "S1b.1", "q1.0", "o0.1", "n0.1", "v1.0", "s1.0", "S1a.1", "p1T.0", "m1.1",
         "a1.0", "a1_stats.0", "E1b.1", "stat1.0", "E1a.1", "y1.0", "S2b.1", "y1T.0", "o1.1", "n1.1", "f.0",
         "S2a.1", "f_stats.0", "m2.1", "stat2.0", "E2b.1", "E2a.1", "y2.0", "y2_stats.0", "h.0", "h_ph.0", "o2.1",
         "n2.1", "q2.0", "q3.0", "proj.1", "v2.0", "proj_stats.1", "pv.0", "x2.1", "x2T.1", "s2.0", "logit.1",
         "chosen.1", "s2_top.0", "topk1.0", "rank.1", "topk2.0", "place.1", "y.1", "yT.1", "select.0", "w.0",
         "q1.1", "sum.0", "v1.1", "sum_stats.0", "s1.1", "x3.0", "p1T.1", "xT.0", "a1.1", "a1_stats.1", "qk0.0",
         "v3.0", "stat1.1", "qk1.0", "y1.1", "qk2.0", "y1T.1", "S0b.0", "f.1", "S0a.0", "f_stats.1", "m0.0",
         "stat2.1", "y2.1", "y2_stats.1", "E0b.0", "E0a.0", "h.1", "S1b.0", "h_ph.1", "o0.0", "q2.1", "q3.1",
         "v2.1", "n0.0", "S1a.0", "pv.1", "m1.0", "s2.1", "s2_top.1", "topk1.1", "topk2.1", "select.1", "E1b.0",
         "E1a.0", "w.1", "S2b.0", "sum.1", "o1.0", "n1.0", "S2a.0", "sum_stats.1", "m2.0", "x3.1", "E2b.0",
         "xT.1", "E2a.0", "qk0.1", "o2.0", "v3.1", "qk1.1", "n2.0", "qk2.1", "proj.0", "proj_stats.0", "S0b.1",
         "x2.0", "S0a.1", "x2T.0", "m0.1", "logit.0", "chosen.0", "E0b.1", "rank.0", "place.0"]


class Round:

    def __init__(self, n, back=0):
        self.n, self.back = n, back

    def times(self, k, plus):
        return self.n * k + (plus - self.back * k)


class At:

    def __init__(self, names):
        self.names, self.next = names, {s: 0 for s in SLOTS}

    def step(self, s, name):
        assert self.names[self.next[s] % len(self.names)] == name, (name, self.names[self.next[s] % len(self.names)])
        self.next[s] += 1
        return 1

    def after(self, n, name):
        return n.times(len(self.names), self.names.index(name) + 1)


def block_kernel(nc, A, out):
    f32, i32, u32 = mybir.dt.float32, mybir.dt.int32, mybir.dt.uint32
    ACT = mybir.ActivationFunctionType
    ALU = mybir.AluOpType
    AX = mybir.AxisListType
    ctx = ExitStack()
    with ctx:
        def sb(name, shape, dt=f32):
            return ctx.enter_context(nc.sbuf_tensor(name, shape, dt))

        def two(name, shape, dt=f32):
            return [sb(f"{name}_{s}", shape, dt) for s in SLOTS]

        def sem(name):
            return ctx.enter_context(nc.semaphore(name))

        const = sb("const", [P, sum(CONSTS.values())])
        K, at = {}, 0
        for name, width in CONSTS.items():
            K[name] = const[:, at:at + width]
            at += width
        ident = K["ident"]
        ids = sb("ids", [P, (B + 2) * NT], i32)
        arena = sb("arena", [P, HC * (4 * (D + 1) + 2 * D)])
        t_wq, t_wk, t_wv, t_w1 = (arena[:, i * HC * (D + 1):(i + 1) * HC * (D + 1)].rearrange("p (c n) -> p c n", c=HC)
                                  for i in range(4))
        t_wo, t_w2 = (arena[:, 4 * HC * (D + 1) + i * HC * D:4 * HC * (D + 1) + (i + 1) * HC * D].rearrange(
            "p (c n) -> p c n", c=HC) for i in range(2))
        e_sizes = (2 * H, HC * D, HC, D)
        e_at = [[h_ * sum(e_sizes) + sum(e_sizes[:i]) for i in range(5)] for h_ in range(2)]
        e_w1, e_w2, e_b1, e_b2 = ([arena[:, e_at[h_][i]:e_at[h_][i + 1]] for h_ in range(2)] for i in range(4))
        bo_row, b2_row = sb("bo_row", [C + 1, D]), sb("b2_row", [C + 1, D])
        a_wq, a_wk, a_wpk = (sb(f"a_{x}", [C, 2, D + 1]) for x in ("wq", "wk", "wpk"))
        m_qk1, m_qk2, m_qpk = (sb(f"m_{x}", [C + 1, 2, D + 1]) for x in ("qk1", "qk2", "qpk"))
        m_vo, m_ff = sb("m_vo", [C + 1, 2, D]), sb("m_ff", [C + 1, 2, D])
        w_v2, w_pv = sb("w_v2", [C + 1, 2, D]), sb("w_pv", [C + 1, 2, D])
        w_qk = sb("w_qk", [C + 1, 2, 2 * NJ * P])
        w_v3 = sb("w_v3", [C + 1, 2, D])
        w_proj = sb("w_proj", [P, NJ, D])
        w_gate = sb("w_gate", [C, 2, NE])
        ln1w, ln1b, ln2w, ln2b = (sb(f"ln{x}", [P, NT * D]) for x in ("1w", "1b", "2w", "2b"))
        affine = sb("affine", [C, 2, 4])
        base = sb("base", [P, B, NT * D])
        gates = sb("gates", [P, B, NT, 2])
        logit_gap = sb("logit_gap", [P, B, NT])
        running = sb("running", [P, NE])
        emb = two("emb", [P, NT, D])
        idx = two("idx", [P, NT], i32)
        y, z, y2, h, hn, x3 = (two(x, [P, NT * D]) for x in ("y", "z", "y2", "h", "hn", "x3"))
        x2 = two("x2", [P, NT, ROW])
        xT = two("xT", [C + 1, 2, S])
        phT = two("phT", [C + 1, 2, S])
        early = two("early", [P, 8 * S + 6 * P + NT * D])
        keys = [early[s][:, 0:NJ * 4 * S].rearrange("p (j i n) -> p j i n", j=NJ, i=4) for s in SLOTS]
        pP, pT = ([early[s][:, (2 * k) * S:(2 * k + 2) * S].rearrange("p (t n) -> p t n", t=NT) for s in SLOTS] for k in range(2))
        pr, qT = ([early[s][0:C + 1, (2 * k) * S:(2 * k + 2) * S].rearrange("p (c n) -> p c n", c=2) for s in SLOTS]
                  for k in range(2, 4))
        sc, sr = ([early[s][:, 8 * S + k * 3 * P:8 * S + (k + 1) * 3 * P] for s in SLOTS] for k in range(2))
        g_f = [early[s][:, 8 * S + 6 * P:] for s in SLOTS]
        vv, pv = two("vv", [P, NT, D]), two("pv", [P, NT, D])
        queries = two("queries", [P, NJ, S])
        vx = two("vx", [P, NT, HEADS, 32])
        prob = two("prob", [P, NT, 4, S])
        mb = two("mb", [P, NT, P])
        sh = two("sh", [P, S])
        on = two("on", [P, NJ, S])
        sm = two("sm", [P, 96])
        top = two("top", [P, 2 * NT, 8])
        ix = two("ix", [P, NT, 8], u32)
        oh = two("oh", [P, 2, NT, NE])
        rk = two("rk", [P, 2, NT, NE])
        lg = two("lg", [P, NT, NE])
        cnt = two("cnt", [P, NT, NE])
        pos_e = two("pos_e", [P, NT, NE])
        slots = two("slots", [P, 2 * NT], u32)
        ps = [ctx.enter_context(nc.psum_tensor(f"ps{s}", [P, 4, 512], f32)) for s in SLOTS]
        dram_x = nc.dram_tensor("expert_rows", [NE * REG, ROW], f32, kind="Internal").ap()
        dram_y = nc.dram_tensor("expert_results", [RESULTS + 2 * STEP, D], f32, kind="Internal").ap()
        idle = sb("idle", [P, NT, ROW])
        table = sb("table", [P, 4 * NE])
        steps_of = sb("steps_of", [P, 3 * NE], i32)
        ex = early[0][:, 0:NT * ROW].rearrange("p (t w) -> p t w", w=ROW)
        eT, ey = xT[0], y[0]
        eh = prob[0][:].rearrange("p t i n -> p (t i) n")
        goes = sb("goes", [P, NT, 2])
        goes_f, goes_to = sb("goes_f", [P, NT]), sb("goes_to", [P, NT], u32)
        back = [early[s][:, k * 4 * D:(k + 1) * 4 * D].rearrange("p (t x) -> p t x", t=NT)
                for s in SLOTS for k in range(BACK // 2)]
        final = [x[s] for x in (z, y2, h, hn) for s in SLOTS]

        def small(s, at, n=1):
            return sm[s][:, at:at + n]

        loaded = sem("weights_loaded")
        consts_loaded = sem("consts_loaded")
        factors = [sem(f"factors_{k}") for k in range(5)]
        fold_mm = sem("fold_products_in_psum")
        fold_cp = sem("fold_products_copied")
        pool_preset, dve_preset = sem("pool_preset"), sem("dve_preset")
        pe_done = [sem(f"pe_done_{s}") for s in SLOTS]
        act_done = [sem(f"act_done_{s}") for s in SLOTS]
        dve_done = [sem(f"dve_done_{s}") for s in SLOTS]
        pool_done = [sem(f"pool_done_{s}") for s in SLOTS]
        gathered = [sem(f"gathered_{s}") for s in SLOTS]
        scattered = [sem(f"scattered_{s}") for s in SLOTS]
        dve_passed, pool_passed, pe_passed = sem("dve_passed"), sem("pool_passed"), sem("pe_passed")
        ranked, idle_written = sem("counts_ready"), sem("idle_rows_written")
        e_loaded = sem("expert_weights_loaded")
        x_loaded, x_turned, xT_ready = sem("x_loaded"), sem("x_turned"), sem("xT_ready")
        h_psum, h_ready, y_psum, y_ready = sem("h_psum"), sem("h_ready"), sem("y_psum"), sem("y_ready")
        y_scattered, y_free, goes_done = sem("y_scattered"), sem("y_free"), sem("goes_done")
        v_chain = sem("vector_chain")
        back_there, back_free, summed, final_stored, final_free = (
            [sem(f"{x}_{k}") for k in range(BACK)] for x in ("back_there", "back_free", "summed", "final_stored", "final_free"))
        gap_exp = sem("gap_exp")

        def each_step(eng, body, first=None):
            eng.wait_ge(ranked, 1)
            with eng.Fori(0, NE // 2) as pair:
                for par in range(2):
                    e = pair * 2 + par
                    count = eng.value_load(steps_of[0:1, bass.ds(e, 1)], min_val=1, max_val=B * S // STEP)
                    before = eng.value_load(steps_of[0:1, bass.ds(e + NE, 1)], min_val=0, max_val=MAX_STEPS - 1)
                    if first is not None:
                        first(par, e, before)
                    with eng.Fori(0, count) as t:
                        body(par, e, t, before + t)

        def total_steps(eng):
            return (eng.value_load(steps_of[0:1, NE - 1:NE], min_val=1, max_val=B * S // STEP)
                    + eng.value_load(steps_of[0:1, 2 * NE - 1:2 * NE], min_val=0, max_val=MAX_STEPS - 1))

        def staggered(eng, chain, now):
            running_chain, stage = {}, {}

            def turns(rounds, names):
                for name, s in names:
                    if name == STAGES[0]:
                        now[s], running_chain[s] = rounds[s], chain(s)
                        stage[s] = next(running_chain[s])
                    if stage.get(s) == name:
                        stage[s] = next(running_chain[s], None)

            order = [(x[:-2], int(x[-1])) for x in TURNS]
            turns((Round(0), Round(0)), order)
            with eng.Fori(1, ROUNDS) as n:
                m = eng.snap(n + 1, min_val=2, max_val=ROUNDS)
                now[1] = Round(m, 2)
                turns((Round(n), Round(m, 1)), order)
            now[0] = now[1] = Round(ROUNDS - 1)
            turns(None, [x for x in order[:order.index((STAGES[0], 1))] if x[1] == 1])

        def by_tile(x, s):
            return x2[s][:, :, 0:D] if x is x2 else x[s][:].rearrange("p (t d) -> p t d", d=D)

        pe_at, act_at, dve_at, pool_at = At(PE_STEPS), At(ACT_STEPS), At(DVE_STEPS), At(POOL_STEPS)

        tower = [(0, t_wq, "t_wq"), (0, t_wk, "t_wk"), (1, t_wv, "t_wv"), (1, t_wo, "t_wo"), (1, bo_row[C:C + 1, :], "bo"),
                 (2, t_w1, "t_w1"), (2, t_w2, "t_w2"), (2, b2_row[C:C + 1, :], "b2"), (3, a_wq, "a_wq"), (3, a_wk, "a_wk"),
                 (4, a_wpk, "a_wpk")]
        rest = [(w_v2, "w_v2"), (w_pv, "w_pv"), (w_qk, "w_qk"), (w_v3, "w_v3"), (w_proj, "w_proj"), (w_gate, "w_gate"),
                (ln1w, "ln1w"), (ln1b, "ln1b"), (ln2w, "ln2w"), (ln2b, "ln2b"), (affine, "affine")]
        block = ctx.enter_context(nc.Block())

        @block.sync
        def _(sp):
            for k, dst, name in tower:
                sp.dma_start(dst if name in ("bo", "b2") else dst[:], A[name]).then_inc(factors[k], 16)
            sp.dma_start(ids[:], A["ids"]).then_inc(consts_loaded, 16)
            sp.dma_start(const[:], A["const"]).then_inc(consts_loaded, 16)
            for dst, name in rest:
                if name.startswith("w_") and name not in ("w_proj", "w_gate"):
                    sp.dma_start(dst[0:C, 0, :], A[name][0:C, :]).then_inc(loaded, 16)
                    sp.dma_start(dst[:, 1, :], A[name][C:2 * C + 1, :]).then_inc(loaded, 16)
                else:
                    sp.dma_start(dst[:], A[name]).then_inc(loaded, 16)
            sp.wait_ge(pool_preset, 1)
            for e in range(NE):
                sp.dma_start(dram_x[e * REG:e * REG + STEP, :].rearrange("(t p) w -> p t w", p=P),
                             idle[:]).then_inc(idle_written, 16)
            for s in SLOTS:
                sp.wait_ge(scattered[s], 64 * ROUNDS)
            first_row = {}

            def find_rows(par, e, g):
                first_row[par] = sp.value_load(steps_of[0:1, bass.ds(e + 2 * NE, 1)], min_val=0, max_val=NE * REG - STEP)

            def load_rows(par, e, t, g):
                sp.wait_ge(xT_ready, g + 1)
                row = nc.s_assert_within(first_row[par] + t * STEP, 0, NE * REG - STEP, skip_runtime_bounds_check_because=(
                    "an expert's steps end at the last row of its region and begin at the idle rows at the earliest"))
                sp.dma_start(ex, dram_x[bass.ds(row, STEP), :].rearrange("(t p) w -> p t w", p=P)).then_inc(x_loaded, 16)

            each_step(sp, load_rows, find_rows)
            sp.wait_ge(xT_ready, total_steps(sp) + 1)
            sp.dma_start(ex, dram_x[0:STEP, :].rearrange("(t p) w -> p t w", p=P)).then_inc(x_loaded, 16)
            with sp.Fori(0, B // BACK) as n:
                for k in range(BACK):
                    sp.wait_ge(summed[k], n + 1)
                    sp.dma_start(out[bass.ds(n * BACK + k, 1), :, :].rearrange("b (t p) d -> p (b t) d", p=P),
                                 final[k][:].rearrange("p (t d) -> p t d", d=D)).then_inc(final_stored[k], 16)
                for k in range(BACK):
                    sp.wait_ge(final_stored[k], (n + 1) * 16)
                    sp.sem_inc(final_free[k], 1)
            for k in range(BACK):
                sp.wait_ge(final_stored[k], B // BACK * 16)
            for s in SLOTS:
                sp.wait_ge(gathered[s], 32 * (ROUNDS + 1))
            sp.wait_ge(e_loaded, 64 * (NE + 1))

        n_loaded = 16 * (len(rest) + 4)

        def products(lhsT, rhs, n_chunks, width, banks):
            for half in range(2):
                for k in range(n_chunks):
                    last = nc.tensor.matmul(ps[0][0:C + 1, banks + half, 0:width],
                                            lhsT[:, k, half * C:half * C + C + 1], rhs[:, k, 0:width],
                                            start=(k == 0), stop=(k == n_chunks - 1))
            return last

        folds = [(t_wq, t_wk, HC, D + 1, m_qk1, None), (t_wv, t_wo, HC, D, m_vo, bo_row), (t_w1, t_w2, HC, D, m_ff, b2_row),
                 (a_wq, a_wk, 2, D + 1, m_qk2, None), (a_wq, a_wpk, 2, D + 1, m_qpk, None)]

        @block.tensor
        def _(pe):
            for k, (lhsT, rhs, n_chunks, width, _, _) in enumerate(folds):
                pe.wait_ge(factors[k], 16 * sum(x[0] == k for x in tower))
                if k > 1:
                    pe.wait_ge(fold_cp, k - 1)
                products(lhsT, rhs, n_chunks, width, k % 2 * 2).then_inc(fold_mm, 1)
            pe.wait_ge(fold_cp, len(folds))
            pe.wait_ge(loaded, n_loaded)
            pe.wait_ge(consts_loaded, 32)
            pe.wait_ge(pool_preset, 1 + len(SLOTS))
            pe.wait_ge(dve_preset, 3)

            def transposes(s, src, bank):
                v = by_tile(src, s)
                for c in range(2):
                    for t in range(NT):
                        last = nc.tensor.transpose(ps[s][0:C, bank, c * S + t * P:c * S + (t + 1) * P],
                                                   v[:, t, c * C:(c + 1) * C], ident)
                return last

            def project_T(s, w, act, bank):
                for m in range(2):
                    for c in range(2):
                        last = nc.tensor.matmul(ps[s][0:C + 1, bank, m * S:(m + 1) * S],
                                                w[0:CK[c], c, m * C:m * C + C + 1], act[s][0:CK[c], c, :],
                                                start=(c == 0), stop=(c == 1))
                return last

            def project(s, w, act, bank, rows=CK, width=D):
                for t in range(NT):
                    for c in range(2):
                        last = nc.tensor.matmul(ps[s][:, bank, t * width:(t + 1) * width],
                                                act[s][0:rows[c], c, t * P:(t + 1) * P], w[0:rows[c], c, :],
                                                start=(c == 0), stop=(c == 1))
                return last

            now = {}

            def dve(s, name):
                pe.wait_ge(dve_done[s], dve_at.after(now[s], name))

            def act(s, name):
                pe.wait_ge(act_done[s], act_at.after(now[s], name))

            def chain(s):
                yield "yT"
                dve(s, "y")
                transposes(s, y, 0).then_inc(pe_done[s], pe_at.step(s, "yT"))
                yield "q1"
                act(s, "yT")
                project_T(s, m_qk1, xT, 1).then_inc(pe_done[s], pe_at.step(s, "q1"))
                yield "v1"
                project(s, m_vo, xT, 2).then_inc(pe_done[s], pe_at.step(s, "v1"))
                yield "s1"
                dve(s, "q1")
                for t in range(NT):
                    for c in range(2):
                        last = nc.tensor.matmul(ps[s][:, 3, t * S:(t + 1) * S], qT[s][0:CK[c], c, t * P:(t + 1) * P],
                                                xT[s][0:CK[c], c, :], start=(c == 0), stop=(c == 1))
                last.then_inc(pe_done[s], pe_at.step(s, "s1"))
                yield "p1T"
                act(s, "p1")
                for k in range(NT):
                    for t in range(NT):
                        last = nc.tensor.transpose(ps[s][:, 0, k * S + t * P:k * S + (t + 1) * P],
                                                   pP[s][:, t, k * P:(k + 1) * P], ident)
                last.then_inc(pe_done[s], pe_at.step(s, "p1T"))
                yield "a1"
                dve(s, "p1T")
                for t in range(NT):
                    for k in range(NT):
                        last = nc.tensor.matmul(ps[s][:, 1, t * D:(t + 1) * D], pT[s][:, k, t * P:(t + 1) * P],
                                                vv[s][:, k, :], start=(k == 0), stop=(k == NT - 1))
                last.then_inc(pe_done[s], pe_at.step(s, "a1"))
                yield "stat1"
                dve(s, "sq1")
                nc.tensor.matmul(ps[s][:, 2, 0:2], K["mean"], small(s, 8, 2), start=True,
                                 stop=True).then_inc(pe_done[s], pe_at.step(s, "stat1"))
                yield "y1T"
                dve(s, "y1")
                transposes(s, y, 0).then_inc(pe_done[s], pe_at.step(s, "y1T"))
                yield "f"
                act(s, "y1T")
                project(s, m_ff, xT, 3).then_inc(pe_done[s], pe_at.step(s, "f"))
                yield "stat2"
                dve(s, "sq2")
                nc.tensor.matmul(ps[s][:, 2, 0:2], K["mean"], small(s, 8, 2), start=True,
                                 stop=True).then_inc(pe_done[s], pe_at.step(s, "stat2"))
                yield "h"
                dve(s, "h")
                transposes(s, h, 0).then_inc(pe_done[s], pe_at.step(s, "hT"))
                hv = h[s][:].rearrange("p (t d) -> p t d", d=D)
                for c in range(2):
                    for t, lo, hi in ((0, 0, P + 1), (1, P + 1, S)):
                        last = nc.tensor.matmul(ps[s][0:C, 1, c * S + lo:c * S + hi], hv[:, t, c * C:(c + 1) * C],
                                                K["phrase"][:, lo:hi], start=True, stop=True)
                last.then_inc(pe_done[s], pe_at.step(s, "ph"))
                yield "q2"
                act(s, "hT")
                project_T(s, m_qk2, xT, 2).then_inc(pe_done[s], pe_at.step(s, "q2"))
                yield "q3"
                project_T(s, m_qpk, xT, 3).then_inc(pe_done[s], pe_at.step(s, "q3"))
                yield "v2"
                project(s, w_v2, xT, 0).then_inc(pe_done[s], pe_at.step(s, "v2"))
                yield "pv"
                dve(s, "ph")
                project(s, w_pv, phT, 1).then_inc(pe_done[s], pe_at.step(s, "pv"))
                yield "s2"
                dve(s, "prod")
                for t in range(NT):
                    for c in range(2):
                        last = nc.tensor.matmul(ps[s][:, 3, t:t + 1], pr[s][0:CK[c], c, t * P:(t + 1) * P],
                                                K["ones"][0:CK[c], 0:1], start=(c == 0), stop=(c == 1))
                last.then_inc(pe_done[s], pe_at.step(s, "phr"))
                for t in range(NT):
                    for c in range(2):
                        last = nc.tensor.matmul(ps[s][:, 2, t * P:t * P + (t + 1) * P], qT[s][0:CK[c], c, t * P:(t + 1) * P],
                                                xT[s][0:CK[c], c, 0:(t + 1) * P], start=(c == 0), stop=(c == 1))
                last.then_inc(pe_done[s], pe_at.step(s, "s2"))
                yield "w"
                dve(s, "w")
                for k in range(3):
                    last = nc.tensor.transpose(ps[s][:, 3, k * P:(k + 1) * P], sc[s][:, k * P:(k + 1) * P], ident)
                last.then_inc(pe_done[s], pe_at.step(s, "wT"))
                yield "sum"
                act(s, "wT")
                nc.tensor.matmul(ps[s][:, 2, 0:D], sr[s][:, 0:P], vv[s][:, 0, :], start=True, stop=True)
                for k in range(NT):
                    last = nc.tensor.matmul(ps[s][:, 2, D:2 * D], sr[s][:, (k + 1) * P:(k + 2) * P], vv[s][:, k, :],
                                            start=(k == 0), stop=(k == NT - 1))
                last.then_inc(pe_done[s], pe_at.step(s, "sum"))
                yield "xT"
                dve(s, "x3")
                transposes(s, h, 0).then_inc(pe_done[s], pe_at.step(s, "xT"))
                for j in range(NJ):
                    yield f"qk{j}"
                    if j == 0:
                        act(s, "xT")
                    for r in range(2):
                        for c in range(2):
                            last = nc.tensor.matmul(ps[s][:, QK_BANK[j], r * S:(r + 1) * S],
                                                    w_qk[0:CK[c], c, (2 * j + r) * P:(2 * j + r + 1) * P],
                                                    xT[s][0:CK[c], c, :], start=(c == 0), stop=(c == 1))
                    last.then_inc(pe_done[s], pe_at.step(s, f"qk{j}"))
                    if j == 0:
                        yield "v3"
                        project(s, w_v3, xT, 3).then_inc(pe_done[s], pe_at.step(s, "v3"))
                def scores(j, t):
                    for i in (0, 2):
                        last = nc.tensor.matmul(ps[s][:, 2 * t + i // 2, :], queries[s][:, j, t * P:(t + 1) * P],
                                                keys[s][:, j, i:i + 2, :].rearrange("p i n -> p (i n)"),
                                                start=True, stop=True)
                    last.then_inc(pe_done[s], pe_at.step(s, f"S{j}{'ab'[t]}"))

                def shifted_scores(j, t):
                    for i in range(4):
                        last = nc.tensor.matmul(ps[s][:, 2 * t + i // 2, i % 2 * S:(i % 2 + 1) * S],
                                                keys[s][:, j, i, t * P:(t + 1) * P], queries[s][:, j, :],
                                                start=True, stop=True)
                    last.then_inc(pe_done[s], pe_at.step(s, f"E{j}{'ab'[t]}"))

                def outputs(j):
                    act(s, f"P{j}a")
                    for t in range(NT):
                        for i in range(4):
                            last = nc.tensor.matmul(ps[s][32 * i:32 * i + 32, 0, 0:S], vx[s][:, t, 4 * j + i, :],
                                                    prob[s][:, t, i, :], start=(t == 0), stop=(t == NT - 1))
                    last.then_inc(pe_done[s], pe_at.step(s, f"o{j}"))

                for j in range(NJ):
                    yield f"S{j}b"
                    if j == 0:
                        dve(s, "qk0")
                        act(s, "v3")
                    else:
                        act(s, f"P{j - 1}b")
                    scores(j, 1)
                    if j:
                        yield f"o{j - 1}"
                        outputs(j - 1)
                    yield f"S{j}a"
                    if j:
                        act(s, f"oc{j - 1}")
                    else:
                        act(s, "qk1")
                        dve(s, "qk2")
                    scores(j, 0)
                    yield f"m{j}"
                    dve(s, f"max{j}a")
                    for t in range(NT):
                        last = nc.tensor.transpose(ps[s][:, 0, t * P:(t + 1) * P], mb[s][:, t, :], ident)
                    last.then_inc(pe_done[s], pe_at.step(s, f"m{j}"))
                    yield f"E{j}b"
                    dve(s, f"qm{j}")
                    shifted_scores(j, 1)
                    yield f"E{j}a"
                    shifted_scores(j, 0)
                yield f"o{NJ - 1}"
                outputs(NJ - 1)
                yield "proj"
                dve(s, "on2")
                for t in range(NT):
                    for j in range(NJ):
                        last = nc.tensor.matmul(ps[s][:, 1, t * D:(t + 1) * D], on[s][:, j, t * P:(t + 1) * P],
                                                w_proj[:, j, :], start=(j == 0), stop=(j == NJ - 1))
                last.then_inc(pe_done[s], pe_at.step(s, "proj"))
                yield "x2T"
                dve(s, "x2")
                transposes(s, x2, 0).then_inc(pe_done[s], pe_at.step(s, "x2T"))
                yield "logit"
                act(s, "x2T")
                project(s, w_gate, xT, 2, rows=(C, C), width=NE).then_inc(pe_done[s], pe_at.step(s, "logit"))
                yield "rank"
                dve(s, "cnt")
                r = ps[s][:, 3, 0:3 * NE]
                nc.tensor.matmul(r[:, 0:NE], K["before"], cnt[s][:, 0, :], start=True, stop=True)
                nc.tensor.matmul(r[:, NE:2 * NE], K["before"], cnt[s][:, 1, :], start=True, stop=False)
                nc.tensor.matmul(r[:, NE:2 * NE], K["ones"], cnt[s][:, 0, :], start=False, stop=True)
                nc.tensor.matmul(r[:, 2 * NE:3 * NE], K["ones"], cnt[s][:, 0, :], start=True, stop=False)
                nc.tensor.matmul(r[:, 2 * NE:3 * NE], K["ones"], cnt[s][:, 1, :], start=False,
                                 stop=True).then_inc(pe_done[s], pe_at.step(s, "rank"))

            staggered(pe, chain, now)


            def turn():
                for c in range(2):
                    for t in range(NT):
                        last = nc.tensor.transpose(ps[1][0:C, 2, c * S + t * P:c * S + (t + 1) * P],
                                                   ex[:, t, c * C:(c + 1) * C], ident)
                last.then_inc(x_turned, 1)

            pe.wait_ge(x_loaded, 16)
            turn()
            pe.sem_inc(y_psum, 1)

            def weights(par, e, g):
                pe.wait_ge(e_loaded, e * 64 + 64)
                pe.sem_inc(pe_passed, 1)

            def step(par, e, t, g):
                def up(k):
                    w = e_w1[par][0:C, :].rearrange("p (c n) -> p c n", c=2)
                    for c in range(2):
                        last = nc.tensor.matmul(ps[0][:, k % 4, 0:STEP], w[:, c, k * P:(k + 1) * P], eT[0:C, c, :],
                                                start=(c == 0), stop=(c == 1))
                    last.then_inc(h_psum, 1)

                def down(k):
                    pe.wait_ge(h_ready, g * HC + (k + 1))
                    w = e_w2[par].rearrange("p (c n) -> p c n", c=HC)
                    for t_ in range(NT):
                        last = nc.tensor.matmul(ps[1][:, t_, 0:D], eh[:, k, t_ * P:(t_ + 1) * P], w[:, k, :],
                                                start=(k == 0), stop=(k == HC - 1))
                    return last

                pe.wait_ge(xT_ready, g + 2)
                up(0)
                for k in range(1, HC):
                    up(k)
                    if k == 1:
                        pe.wait_ge(y_ready, g + 1)
                    if k == HC - 1:
                        pe.wait_ge(x_loaded, g * 16 + 32)
                        turn()
                    down(k - 1)
                down(HC - 1).then_inc(y_psum, 1)

            each_step(pe, step, weights)

        @block.scalar
        def _(act):
            act.wait_ge(loaded, n_loaded)
            now = {}

            def pe(s, name):
                act.wait_ge(pe_done[s], pe_at.after(now[s], name))

            def dve(s, name):
                act.wait_ge(dve_done[s], dve_at.after(now[s], name))

            def copy_T(s, name):
                pe(s, name)
                nc.scalar.copy(xT[s][0:C, :, :], ps[s][0:C, 0, :]).then_inc(act_done[s], act_at.step(s, name))

            def affine_T(s, name, which):
                pe(s, name)
                for c in range(2):
                    last = nc.scalar.activation(xT[s][0:C, c, :], ps[s][0:C, 0, c * S:(c + 1) * S], ACT.Identity,
                                                bias=affine[:, c, which + 1:which + 2], scale=affine[:, c, which:which + 1])
                last.then_inc(act_done[s], act_at.step(s, name))

            def chain(s):
                yield "yT"
                copy_T(s, "yT")
                yield "v1"
                pe(s, "v1")
                nc.scalar.copy(vv[s][:], ps[s][:, 2, 0:NT * D]).then_inc(act_done[s], act_at.step(s, "v1"))
                yield "s1"
                dve(s, "max1")
                for t in range(NT):
                    last = nc.scalar.activation(pP[s][:, t, :], ps[s][:, 3, t * S:(t + 1) * S], ACT.Exp,
                                                bias=small(s, t), accum_out=small(s, 2 + t))
                last.then_inc(act_done[s], act_at.step(s, "p1"))
                yield "y1T"
                copy_T(s, "y1T")
                yield "f"
                pe(s, "f")
                nc.scalar.activation(g_f[s][:], ps[s][:, 3, 0:NT * D], ACT.Gelu).then_inc(
                    act_done[s], act_at.step(s, "gelu"))
                yield "h"
                copy_T(s, "hT")
                yield "v2"
                pe(s, "v2")
                nc.scalar.copy(vv[s][:], ps[s][:, 0, 0:NT * D]).then_inc(act_done[s], act_at.step(s, "v2"))
                yield "pv"
                pe(s, "pv")
                nc.scalar.copy(pv[s][:], ps[s][:, 1, 0:NT * D]).then_inc(act_done[s], act_at.step(s, "pv"))
                yield "s2_top"
                dve(s, "nm")
                nc.scalar.activation(pP[s][:, 0, 0:P], sc[s][:, 0:P], ACT.Exp, bias=small(s, 0))
                nc.scalar.activation(pP[s][:, 1, :], sc[s][:, P:3 * P], ACT.Exp, bias=small(s, 1))
                nc.scalar.activation(small(s, 6), small(s, 4), ACT.Exp, bias=small(s, 0))
                nc.scalar.activation(small(s, 7), small(s, 5), ACT.Exp, bias=small(s, 1)).then_inc(
                    act_done[s], act_at.step(s, "e2"))
                yield "w"
                pe(s, "wT")
                nc.scalar.copy(sr[s][:], ps[s][:, 3, 0:3 * P]).then_inc(act_done[s], act_at.step(s, "wT"))
                yield "xT"
                affine_T(s, "xT", 0)
                yield "v3"
                pe(s, "v3")
                nc.scalar.copy(vx[s][:, :, :, 0:HD],
                               ps[s][:, 3, 0:NT * D].rearrange("p (t h d) -> p t h d", t=NT, h=HEADS)).then_inc(
                    act_done[s], act_at.step(s, "v3"))
                yield "qk1"
                pe(s, "qk1")
                for i in range(4):
                    nc.scalar.activation(keys[s][:, 1, i, :], ps[s][:, QK_BANK[1], 0:S], ACT.Copy, scale=K["head"][:, i:i + 1])
                nc.scalar.copy(queries[s][:, 1, :], ps[s][:, QK_BANK[1], S:2 * S]).then_inc(act_done[s], act_at.step(s, "qk1"))
                def output(j):
                    pe(s, f"o{j}")
                    nc.scalar.copy(on[s][:, j, :], ps[s][:, 0, 0:S]).then_inc(act_done[s], act_at.step(s, f"oc{j}"))

                for j in range(NJ):
                    for t in (1, 0):
                        part = f"{j}{'ab'[t]}"
                        yield "E" + part
                        pe(s, "E" + part)
                        nc.scalar.activation(prob[s][:, t, :, :].rearrange("p i n -> p (i n)"),
                                             ps[s][:, 2 * t:2 * t + 2, :].rearrange("p i n -> p (i n)"), ACT.Exp,
                                             scale=HD ** -0.5).then_inc(act_done[s], act_at.step(s, "P" + part))
                    yield f"o{j}"
                    output(j)
                yield "x2T"
                affine_T(s, "x2T", 2)
            staggered(act, chain, now)
            for s in SLOTS:
                dve(s, "dg")
            nc.scalar.activation(logit_gap[:], logit_gap[:], ACT.Exp).then_inc(gap_exp, 1)

            def weights(par, e, g):
                act.wait_ge(e_loaded, e * 64 + 64)

            def step(par, e, t, g):
                for k in range(HC):
                    act.wait_ge(h_psum, g * HC + (k + 1))
                    nc.scalar.activation(eh[:, k, :], ps[0][:, k % 4, 0:STEP], ACT.Gelu,
                                         bias=e_b1[par][:, k:k + 1]).then_inc(h_ready, 1)

            each_step(act, step, weights)
            act.wait_ge(y_scattered, total_steps(act) * 32)
            with act.Fori(0, B // BACK) as n:
                for k in range(BACK):
                    act.wait_ge(back_free[k], n + 1)
                    act.dma_start(back[k], dram_y[bass.ds((n * BACK + k) * (2 * S), 2 * S), :].rearrange(
                        "(t p x) d -> p t (x d)", t=NT, p=P)).then_inc(back_there[k], 16)

        @block.gpsimd
        def _(pool):
            for s in SLOTS:
                nc.gpsimd.memset(vx[s][:], 1.0)
                last = nc.gpsimd.memset(mb[s][:], 0.0)
            nc.gpsimd.memset(idle[:], 0.0).then_inc(pool_passed, 1)
            pool.wait_ge(pool_passed, 1)
            pool.wait_ge(consts_loaded, 32)
            nc.gpsimd.tensor_copy(idle[:, :, D], K["idle"]).then_inc(pool_preset, 1)

            def gather(s):
                for t in range(NT):
                    nc.gpsimd.indirect_dma_start(
                        out=emb[s][:, t, :], out_offset=None, in_=A["emb"],
                        in_offset=bass.IndirectOffsetOnAxis(ap=idx[s][:, t:t + 1].bitcast(u32), axis=0)).then_inc(gathered[s], 16)

            def load_expert(e, par):
                for dst, name in ((e_w1[par][0:C, :], "e_w1"), (e_w2[par], "e_w2"), (e_b1[par], "e_b1"), (e_b2[par], "e_b2")):
                    nc.gpsimd.dma_start(dst, A[name][bass.ds(e, 1), :, :].rearrange("e p n -> p (e n)")).then_inc(e_loaded, 16)

            for s in SLOTS:
                nc.gpsimd.tensor_copy(idx[s][:], ids[:, s * NT:(s + 1) * NT]).then_inc(pool_preset, 1)
                pool.wait_ge(pool_preset, 2 + s)
                gather(s)
            pool.wait_ge(fold_cp, len(folds))
            load_expert(0, 0)
            pool.wait_ge(idle_written, 16 * NE)
            now = {}

            def dve(s, name):
                pool.wait_ge(dve_done[s], dve_at.after(now[s], name))

            def rsqrt(s, name, wait, at, width):
                dve(s, wait)
                nc.gpsimd.tensor_tensor(small(s, at + width, width), small(s, at, width), K["power"][:, 0:width],
                                        ALU.pow).then_inc(pool_done[s], pool_at.step(s, name))

            def chain(s):
                yield "y"
                dve(s, "y")
                nc.gpsimd.tensor_copy(idx[s][:], ids[:, bass.ds(now[s].times(2 * NT, (2 + s) * NT), NT)]).then_inc(
                    pool_done[s], pool_at.step(s, "idx"))
                pool.wait_ge(pool_done[s], pool_at.after(now[s], "idx"))
                pool.sem_inc(pool_passed, 1)
                gather(s)
                yield "stat1"
                rsqrt(s, "r1", "ve1", 14, 1)
                yield "stat2"
                rsqrt(s, "r2", "ve2", 14, 1)
                yield "y2_stats"
                rsqrt(s, "r3", "ve3", 20, 2)
                yield "sum_stats"
                rsqrt(s, "r4", "ve4", 24, 4)
                yield "proj_stats"
                rsqrt(s, "r5", "ve5", 20, 2)
                nc.gpsimd.tensor_tensor(base[:, bass.ds(now[s].times(2, s), 1), :].rearrange("p b d -> p (b d)"), hn[s][:], x3[s][:],
                                        ALU.add).then_inc(pool_done[s], pool_at.step(s, "base"))
                yield "place"
                dve(s, "slot")
                pool.sem_inc(pool_passed, 1)
                for k in range(2):
                    for t in range(NT):
                        nc.gpsimd.indirect_dma_start(
                            out=dram_x, out_offset=bass.IndirectOffsetOnAxis(ap=slots[s][:, k * NT + t:k * NT + t + 1], axis=0),
                            in_=x2[s][:, t, :], in_offset=None).then_inc(scattered[s], 16)
                pool.wait_ge(scattered[s], now[s].times(64, 64))
                pool.sem_inc(pool_passed, 1)

            staggered(pool, chain, now)

            pool.sem_inc(y_free, 1)

            def next_weights(par, e, g):
                pool.wait_ge(y_psum, g + 1)
                pool.sem_inc(pool_passed, 1)
                load_expert((e + 1) % NE, 1 - par)

            def scatter(par, e, t, g):
                pool.wait_ge(y_ready, g + 2)
                pool.sem_inc(pool_passed, 1)
                for t_ in range(NT):
                    nc.gpsimd.indirect_dma_start(
                        out=dram_y, out_offset=bass.IndirectOffsetOnAxis(ap=goes_to[:, t_:t_ + 1], axis=0),
                        in_=ey[:, t_ * D:(t_ + 1) * D], in_offset=None).then_inc(y_scattered, 16)
                pool.wait_ge(y_scattered, g * 32 + 32)
                pool.sem_inc(y_free, 1)

            each_step(pool, scatter, next_weights)

        @block.vector
        def _(dve):
            for s in SLOTS:
                nc.vector.memset(xT[s][C:C + 1, :, :], 1.0)
                nc.vector.memset(phT[s][C:C + 1, :, :], 1.0)
                nc.vector.memset(small(s, 94), 0.0)
            dve.wait_ge(consts_loaded, 32)
            nc.vector.tensor_copy(running[:], K["region"]).then_inc(dve_preset, 1)
            for k, (_, _, _, width, dst, bias) in enumerate(folds):
                dve.wait_ge(fold_mm, k + 1)
                scale = float(D) ** -0.5 if k >= 3 else 1.0
                last = nc.vector.tensor_scalar(dst[:, :, 0:width], ps[0][0:C + 1, k % 2 * 2:k % 2 * 2 + 2, 0:width], scale, None, ALU.mult)
                last.then_inc(fold_cp, 1)
                if bias is not None:
                    dve.wait_ge(fold_cp, k + 1)
                    nc.vector.tensor_tensor(dst[C:C + 1, 1, :], dst[C:C + 1, 1, :], bias[C:C + 1, :], ALU.add).then_inc(dve_preset, 1)
            dve.wait_ge(dve_preset, 3)
            dve.wait_ge(pool_preset, 1 + len(SLOTS))
            dve.wait_ge(loaded, n_loaded)
            now = {}

            def pe(s, name):
                dve.wait_ge(pe_done[s], pe_at.after(now[s], name))

            def act(s, name):
                dve.wait_ge(act_done[s], act_at.after(now[s], name))

            def pool(s, name):
                dve.wait_ge(pool_done[s], pool_at.after(now[s], name))

            def mark(ins, s, name):
                ins.then_inc(dve_done[s], dve_at.step(s, name))

            def link(ins, s, name):
                mark(ins, s, name)
                dve.wait_ge(dve_done[s], dve_at.after(now[s], name))

            def plain():
                dve.sem_inc(dve_passed, 1)

            def tile(x, s, t):
                return x[s][:, t * D:(t + 1) * D]

            def sums2d(s, k):
                link(nc.vector.bn_stats(small(s, 32, 6), z[s][:]), s, f"bs{k}")
                mv = small(s, 8, 2)
                plain()
                link(nc.vector.bn_aggr(mv, small(s, 32, 6)), s, f"mv{k}")
                mark(nc.vector.scalar_tensor_tensor(mv[:, 1:2], mv[:, 0:1], mv[:, 0:1], mv[:, 1:2], ALU.mult, ALU.add),
                     s, f"sq{k}")

            def norm2d(s, k, w):
                pe(s, f"stat{k}")
                link(nc.vector.tensor_copy(small(s, 10, 2), ps[s][:, 2, 0:2]), s, f"st{k}")
                link(nc.vector.scalar_tensor_tensor(small(s, 12), small(s, 10), small(s, 10), small(s, 11),
                                                    ALU.mult, ALU.subtract), s, f"nv{k}")
                mark(nc.vector.tensor_scalar(small(s, 14), small(s, 12), -1.0, LN_EPS, ALU.mult, ALU.add), s, f"ve{k}")
                mark(nc.vector.scalar_tensor_tensor(z[s][:], z[s][:], small(s, 10), w[:], ALU.subtract, ALU.mult),
                     s, f"z{k}")

            def norm2d_out(s, k, b, dst):
                pool(s, f"r{k}")
                dve.wait_ge(dve_done[s], dve_at.after(now[s], f"z{k}"))
                link(nc.vector.scalar_tensor_tensor(dst[s][:], z[s][:], small(s, 15), b[:], ALU.mult, ALU.add),
                     s, f"y{k}")

            def row_stats(s, k, src):
                for t in range(NT):
                    last = nc.vector.bn_stats(small(s, 32 + 6 * t, 6), tile(src, s, t))
                link(last, s, f"bs{k}")
                plain()
                for t in range(NT):
                    last = nc.vector.bn_aggr(small(s, 16 + 2 * t, 2), small(s, 32 + 6 * t, 6))
                link(last, s, f"mv{k}")

            def variances(s):
                return sm[s][:, 16:20].rearrange("p (t x) -> p t x", x=2)[:, :, 1]

            def standardise(dst, src, s, r):
                for t in range(NT):
                    last = nc.vector.tensor_scalar(by_tile(dst, s)[:, t, :], tile(src, s, t), small(s, 16 + 2 * t), small(s, r + t),
                                                   ALU.subtract, ALU.mult)
                return last

            def bands(x, s):
                return (x[s][:, 0:P], x[s][:, P:3 * P])

            def chain(s):
                yield "y"
                dve.wait_ge(gathered[s], now[s].times(32, 32))
                mark(nc.vector.tensor_tensor(y[s][:], emb[s][:].rearrange("p t d -> p (t d)"), K["pos"], ALU.add), s, "y")
                yield "q1"
                pe(s, "q1")
                mark(nc.vector.tensor_copy(flat(qT[s]), ps[s][0:C + 1, 1, :]), s, "q1")
                yield "s1"
                pe(s, "s1")
                mark(nc.vector.tensor_reduce(small(s, 0, 2), ps[s][:, 3, :].rearrange("p (t n) -> p t n", t=NT),
                                             AX.X, ALU.max, negate=True), s, "max1")
                yield "p1T"
                pe(s, "p1T")
                mark(nc.vector.tensor_copy(flat(pT[s]), ps[s][:, 0, :]), s, "p1T")
                act(s, "p1")
                link(nc.vector.reciprocal(small(s, 4, 2), small(s, 2, 2)), s, "rr")
                yield "a1"
                pe(s, "a1")
                for t in range(NT):
                    last = nc.vector.scalar_tensor_tensor(tile(z, s, t), ps[s][:, 1, t * D:(t + 1) * D], small(s, 4 + t),
                                                          tile(y, s, t), ALU.mult, ALU.add)
                link(last, s, "R1")
                yield "a1_stats"
                sums2d(s, 1)
                yield "stat1"
                norm2d(s, 1, ln1w)
                yield "y1"
                norm2d_out(s, 1, ln1b, y)
                yield "f"
                act(s, "gelu")
                link(nc.vector.tensor_tensor(z[s][:], y[s][:], g_f[s][:], ALU.add), s, "R2")
                yield "f_stats"
                sums2d(s, 2)
                yield "stat2"
                norm2d(s, 2, ln2w)
                yield "y2"
                norm2d_out(s, 2, ln2b, y2)
                yield "y2_stats"
                row_stats(s, 3, y2)
                mark(nc.vector.tensor_scalar(small(s, 20, 2), variances(s), LN_EPS, None, ALU.add), s, "ve3")
                yield "h"
                pool(s, "r3")
                mark(standardise(h, y2, s, 22), s, "h")
                yield "h_ph"
                pe(s, "ph")
                mark(nc.vector.tensor_copy(phT[s][0:C, :, :].rearrange("p c n -> p (c n)"), ps[s][0:C, 1, :]), s, "ph")
                yield "q2"
                pe(s, "q2")
                mark(nc.vector.tensor_copy(flat(qT[s]), ps[s][0:C + 1, 2, :]), s, "q2")
                yield "q3"
                pe(s, "q3")
                dve.wait_ge(dve_done[s], dve_at.after(now[s], "ph"))
                mark(nc.vector.tensor_tensor(flat(pr[s]), ps[s][0:C + 1, 3, :], flat(phT[s]), ALU.mult), s, "prod")
                yield "s2"
                pe(s, "s2")
                nc.vector.tensor_copy(small(s, 4, 2), ps[s][:, 3, 0:NT])
                link(nc.vector.tensor_tensor(sc[s][:], ps[s][:, 2, 0:3 * P], K["mask"], ALU.add), s, "sc")
                yield "s2_top"
                plain()
                for t in range(NT):
                    last = nc.vector.max(top[s][:, t, :], bands(sc, s)[t])
                link(last, s, "t1")
                for t in range(NT):
                    last = nc.vector.tensor_scalar(small(s, t), top[s][:, t, 0:1], small(s, 4 + t), -1.0, ALU.max, ALU.mult)
                mark(last, s, "nm")
                yield "topk1"
                plain()
                for t in range(NT):
                    last = nc.vector.match_replace(bands(sr, s)[t], top[s][:, t, :], bands(sc, s)[t], TAKEN)
                link(last, s, "mr1")
                plain()
                for t in range(NT):
                    last = nc.vector.max(top[s][:, NT + t, :], bands(sr, s)[t])
                link(last, s, "t2")
                yield "topk2"
                plain()
                for t in range(NT):
                    last = nc.vector.match_replace(bands(sr, s)[t], top[s][:, NT + t, :], bands(sr, s)[t], TAKEN)
                link(last, s, "mr2")
                yield "select"
                link(nc.vector.scalar_tensor_tensor(sr[s][:], sr[s][:], TAKEN_BELOW, K["seq"], ALU.is_lt, ALU.add), s, "sel")
                yield "w"
                act(s, "e2")
                e = (pP[s][:, 0, 0:P], pP[s][:, 1, :])
                for t in range(NT):
                    last = nc.vector.scalar_tensor_tensor(bands(sc, s)[t], e[t], 1.0, bands(sr, s)[t], ALU.mult, ALU.mult,
                                                          accum_out=small(s, 52 + t))
                link(last, s, "w")
                link(nc.vector.tensor_tensor(small(s, 52, 2), small(s, 52, 2), small(s, 6, 2), ALU.add), s, "den")
                link(nc.vector.reciprocal(small(s, 54, 2), small(s, 52, 2)), s, "rden")
                link(nc.vector.tensor_tensor(small(s, 54, 2), small(s, 54, 2), K["real"], ALU.mult), s, "real")
                yield "sum"
                pe(s, "sum")
                for t in range(NT):
                    last = nc.vector.scalar_tensor_tensor(tile(h, s, t), pv[s][:, t, :], small(s, 6 + t),
                                                          ps[s][:, 2, t * D:(t + 1) * D], ALU.mult, ALU.add)
                link(last, s, "u")
                for t in range(NT):
                    last = nc.vector.scalar_tensor_tensor(tile(hn, s, t), tile(h, s, t), small(s, 54 + t), tile(y2, s, t),
                                                          ALU.mult, ALU.add)
                link(last, s, "hn")
                yield "sum_stats"
                row_stats(s, 4, hn)
                nc.vector.tensor_scalar(small(s, 24, 2), variances(s), LN_EPS, None, ALU.add)
                mark(nc.vector.tensor_scalar(small(s, 26, 2), variances(s), 1.0 + LN_EPS, LN_EPS * LN_EPS, ALU.mult, ALU.add),
                     s, "ve4")
                yield "x3"
                pool(s, "r4")
                standardise(h, hn, s, 30)
                mark(standardise(x3, hn, s, 28), s, "x3")
                for j in (0, 2):
                    yield f"qk{j}"
                    pe(s, f"qk{j}")
                    nc.vector.tensor_tensor(keys[s][:, j, :, :], ps[s][:, QK_BANK[j], 0:S].unsqueeze(1).to_broadcast([P, 4, S]),
                                            K["head"].unsqueeze(2).to_broadcast([P, 4, S]), ALU.mult)
                    mark(nc.vector.tensor_copy(queries[s][:, j, :], ps[s][:, QK_BANK[j], S:2 * S]), s, f"qk{j}")
                def maxima(j, t):
                    part = f"{j}{'ab'[t]}"
                    pe(s, "S" + part)
                    mark(nc.vector.tensor_reduce(mb[s][:, t, :].rearrange("p (i x) -> p i x", x=32)[:, :, HD],
                                                 ps[s][:, 2 * t:2 * t + 2, :].rearrange("p h (i n) -> p (h i) n", n=S),
                                                 AX.X, ALU.max), s, "max" + part)

                def normalise(j):
                    act(s, f"oc{j}")
                    plain()
                    link(nc.vector.stream_shuffle(sh[s][:], on[s][:, j, :], [HD + i % HD for i in range(32)]), s, f"sh{j}")
                    link(nc.vector.reciprocal(sh[s][:], sh[s][:]), s, f"rc{j}")
                    yield f"n{j}"
                    mark(nc.vector.tensor_tensor(on[s][:, j, :], on[s][:, j, :], sh[s][:], ALU.mult), s, f"on{j}")

                for j in range(NJ):
                    yield f"S{j}b"
                    maxima(j, 1)
                    if j:
                        yield f"o{j - 1}"
                        yield from normalise(j - 1)
                    yield f"S{j}a"
                    maxima(j, 0)
                    yield f"m{j}"
                    pe(s, f"m{j}")
                    q = queries[s][:, j, :]
                    mark(nc.vector.tensor_tensor(q, ps[s][:, 0, 0:S], q, ALU.add), s, f"qm{j}")
                yield f"o{NJ - 1}"
                yield from normalise(NJ - 1)
                yield "proj"
                pe(s, "proj")
                link(nc.vector.tensor_tensor(x3[s][:], ps[s][:, 1, 0:NT * D], x3[s][:], ALU.add), s, "xx")
                yield "proj_stats"
                row_stats(s, 5, x3)
                mark(nc.vector.tensor_scalar(small(s, 20, 2), variances(s), LN_EPS, None, ALU.add), s, "ve5")
                yield "x2"
                pool(s, "r5")
                mark(standardise(x2, x3, s, 22), s, "x2")
                nc.vector.tensor_copy(x2[s][:, :, D], K["place"][:, bass.ds(now[s].times(2 * NT, s * NT), NT)])
                yield "logit"
                pe(s, "logit")
                link(nc.vector.tensor_copy(flat(lg[s]), ps[s][:, 2, 0:NT * NE]), s, "lg")
                plain()
                for t in range(NT):
                    last = nc.vector.max(top[s][:, t, :], lg[s][:, t, :])
                link(last, s, "top")
                plain()
                for t in range(NT):
                    last = nc.vector.max_index(ix[s][:, t, :], top[s][:, t, :], lg[s][:, t, :])
                link(last, s, "ix")
                yield "chosen"
                chosen = small(s, 56, 4).rearrange("p (k t) -> p k t", k=2)
                link(nc.vector.tensor_copy(chosen, ix[s][:, :, 0:2].rearrange("p t k -> p k t")), s, "ixf")
                nc.vector.tensor_copy(x2[s][:, :, D + 1], chosen[:, 0, :])
                for k in range(2):
                    last = nc.vector.tensor_tensor(oh[s][:, k, :, :], K["expert"].unsqueeze(1).to_broadcast([P, NT, NE]),
                                                   chosen[:, k, :].unsqueeze(2).to_broadcast([P, NT, NE]), ALU.is_equal)
                link(last, s, "oh")
                mark(nc.vector.tensor_tensor(flat(cnt[s]), flat(oh[s][:, 0, :, :]), flat(oh[s][:, 1, :, :]), ALU.add), s, "cnt")
                mark(nc.vector.tensor_tensor(logit_gap[:, bass.ds(now[s].times(2, s), 1), :].rearrange("p b t -> p (b t)"), top[s][:, 0:NT, 1], top[s][:, 0:NT, 0], ALU.subtract), s, "dg")
                yield "rank"
                pe(s, "rank")
                link(nc.vector.tensor_tensor(pos_e[s][:], ps[s][:, 3, 0:NT * NE].rearrange("p (t e) -> p t e", t=NT),
                                             running[:].unsqueeze(1).to_broadcast([P, NT, NE]), ALU.add), s, "pos")
                link(nc.vector.tensor_tensor(running[:], ps[s][:, 3, NT * NE:3 * NE], running[:], ALU.add), s, "run")
                yield "place"
                link(nc.vector.tensor_tensor(rk[s][:], oh[s][:], pos_e[s][:].unsqueeze(1).to_broadcast([P, 2, NT, NE]),
                                             ALU.mult), s, "pick")
                link(nc.vector.tensor_reduce(small(s, 60, 4), rk[s][:].rearrange("p k t e -> p (k t) e"), AX.X, ALU.add),
                     s, "slotf")
                mark(nc.vector.tensor_copy(slots[s][:], small(s, 60, 4)), s, "slot")

            staggered(dve, chain, now)

            v_links = [0]

            def link_v(ins):
                v_links[0] += 1
                ins.then_inc(v_chain, 1)
                dve.wait_ge(v_chain, v_links[0])

            filled, steps_f, upto = (table[:, k * NE:(k + 1) * NE] for k in range(3))
            link_v(nc.vector.tensor_tensor(filled, running[:], K["region"], ALU.subtract))
            link_v(nc.vector.tensor_scalar(filled, filled, 1.0, float(STEP - 1), ALU.max, ALU.add))
            link_v(nc.vector.tensor_copy(steps_of[:, NE:2 * NE], filled))
            link_v(nc.vector.tensor_scalar(steps_of[:, 0:NE], steps_of[:, NE:2 * NE], STEP.bit_length() - 1, None,
                                           ALU.logical_shift_right))
            link_v(nc.vector.tensor_copy(steps_f, steps_of[:, 0:NE]))
            link_v(nc.vector.tensor_tensor_scan(upto, K["ones"][:, 0:NE], steps_f, 0.0, ALU.mult, ALU.add))
            link_v(nc.vector.tensor_tensor(upto, upto, steps_f, ALU.subtract))
            link_v(nc.vector.scalar_tensor_tensor(filled, steps_f, float(-STEP), running[:], ALU.mult, ALU.add))
            nc.vector.tensor_copy(steps_of[:, 2 * NE:3 * NE], filled)
            nc.vector.tensor_copy(steps_of[:, NE:2 * NE], upto).then_inc(ranked, 1)
            dve.sem_inc(xT_ready, 1)
            dve.sem_inc(y_ready, 1)

            def spread(g):
                dve.wait_ge(x_turned, g + 1)
                nc.vector.tensor_copy(goes[:], ex[:, :, D:ROW])
                for c in range(2):
                    last = nc.vector.tensor_scalar(eT[0:C, c, :], ps[1][0:C, 2, c * S:(c + 1) * S], affine[:, c, 2:3],
                                                   affine[:, c, 3:4], ALU.mult, ALU.add)
                last.then_inc(xT_ready, 1)

            def weights(par, e, g):
                dve.wait_ge(e_loaded, e * 64 + 64)
                dve.sem_inc(dve_passed, 1)

            def step(par, e, t, g):
                dve.wait_ge(xT_ready, g + 2)
                dve.wait_ge(y_ready, g + 1)
                dve.sem_inc(dve_passed, 1)
                nc.vector.scalar_tensor_tensor(goes_f[:], goes[:, :, 1], K["expert"][:, bass.ds(e, 1)], goes[:, :, 0],
                                               ALU.not_equal, ALU.add).then_inc(goes_done, 1)
                dve.wait_ge(goes_done, g + 1)
                spread(g + 1)
                dve.wait_ge(y_psum, g + 2)
                dve.wait_ge(y_free, g + 1)
                nc.vector.tensor_tensor(ey[:].rearrange("p (t d) -> p t d", d=D), ps[1][:, 0:2, 0:D],
                                        e_b2[par].unsqueeze(1).to_broadcast([P, NT, D]), ALU.add)
                nc.vector.tensor_copy(goes_to[:], goes_f[:]).then_inc(y_ready, 1)

            spread(0)
            for s in SLOTS:
                pool(s, "base")
            dve.wait_ge(gap_exp, 1)
            link_v(nc.vector.tensor_scalar(gates[:, :, :, 1], logit_gap[:], 1.0, None, ALU.add))
            link_v(nc.vector.reciprocal(gates[:, :, :, 0], gates[:, :, :, 1]))
            link_v(nc.vector.tensor_tensor(gates[:, :, :, 1], logit_gap[:], gates[:, :, :, 0], ALU.mult))
            each_step(dve, step, weights)
            for k in range(BACK):
                dve.sem_inc(back_free[k], 1)
                dve.sem_inc(final_free[k], 1)
            with dve.Fori(0, B // BACK) as n:
                for first in range(0, BACK, 2):
                    for choice in range(2):
                        for k in (first, first + 1):
                            if choice == 0:
                                dve.wait_ge(back_there[k], (n + 1) * 16)
                                dve.wait_ge(final_free[k], n + 1)
                            else:
                                dve.wait_ge(v_chain, n * BACK + (v_links[0] + 1 + k))
                            for t in range(NT):
                                g_ = gates[:, bass.ds(n * BACK + k, 1), t, choice:choice + 1].rearrange("p b k -> p (b k)")
                                acc = final[k][:, t * D:(t + 1) * D]
                                old = base[:, bass.ds(n * BACK + k, 1), t * D:(t + 1) * D].rearrange("p b d -> p (b d)")
                                last = nc.vector.scalar_tensor_tensor(acc, back[k][:, t, choice * D:(choice + 1) * D], g_,
                                                                      acc if choice else old, ALU.mult, ALU.add)
                            last.then_inc(summed[k] if choice else v_chain, 1)
                    for k in (first, first + 1):
                        dve.wait_ge(summed[k], n + 1)
                        dve.sem_inc(back_free[k], 1)


def flat(x):
    x = x[:] if not isinstance(x, bass.AP) else x
    return x.rearrange("p a b -> p (a b)")


def constants(np):
    p = np.arange(P)[:, None]
    f = np.float32
    c = {"ident": np.eye(P), "ones": np.ones((P, P)), "mean": np.full((P, P), 1.0 / P), "before": p < np.arange(P)[None, :]}
    pos = np.arange(S, dtype=f)[:, None]
    i = np.arange(D, dtype=f)[None, :]
    ang = pos / np.power(f(10000.0), i / f(D))
    enc = np.where(np.arange(D)[None, :] % 2 == 0, np.sin(ang), np.cos(ang)).astype(f)
    c["pos"] = enc.reshape(NT, P, D).transpose(1, 0, 2).reshape(P, NT * D)
    s = np.arange(2 * P)[None, :]
    c["mask"] = np.concatenate([np.where(s[:, :P] < p, 0.0, MASKED), np.where((s >= p) & (s < p + P), 0.0, MASKED)], 1)
    c["seq"] = np.concatenate([s[:, :P] == p - 1, s == p + P - 1], 1)
    ph = np.zeros((P, S))
    for t in range(1, S):
        first = (t - 1) // CHUNK * CHUNK
        own = 0 if t <= P else P
        ph[first - own:t - own, t] = 1.0 / (t - first)
    c["phrase"] = ph
    c["real"] = np.stack([np.arange(P) > 0, np.ones(P)], 1)
    c["head"] = np.arange(P)[:, None] // 32 == np.arange(4)[None, :]
    c["expert"] = np.tile(np.arange(NE), (P, 1))
    c["region"] = np.tile(np.arange(NE) * REG + STEP, (P, 1))
    c["place"] = 2 * (np.arange(B * NT)[None, :] * P + p)
    c["idle"] = RESULTS + 2 * (np.arange(NT)[None, :] * P + p)
    c["power"] = np.full((P, 4), -0.5)
    return np.concatenate([c[name].astype(f) for name in CONSTS], 1)


def layouts(np, inp):
    g = {k: np.ascontiguousarray(v) for k, v in inp.items()}
    f = np.float32
    rows = lambda w, b: np.concatenate([w, b[None, :]], 0)
    hid = lambda w: w.reshape(HC, P, -1).transpose(1, 0, 2)
    a = {"const": constants(np)}
    ids = np.zeros(((B + 2) * NT, P), np.int32)
    ids[:B * NT] = g["x"].reshape(B * NT, P)
    a["ids"] = ids.T
    a["emb"] = g["L0_tok_emb"]
    t, n, m = "L0_tok_", "L0_attn_", "L0_ffn_"
    a["t_wq"], a["t_wk"], a["t_wv"], a["t_w1"] = (hid(rows(g[t + w], g[t + b]).T) for w, b in
                                                 (("Wq", "bq"), ("Wk", "bk"), ("Wv", "bv"), ("W1", "b1")))
    a["t_wo"], a["t_w2"] = hid(g[t + "Wo"]), hid(g[t + "W2"])
    a["bo"], a["b2"] = g[t + "bo"][None, :], g[t + "b2"][None, :]
    a["a_wq"], a["a_wk"], a["a_wpk"] = (rows(g[n + w], g[n + b]).T.reshape(2, C, D + 1).transpose(1, 0, 2) for w, b in
                                        (("Wq", "bq"), ("Wk", "bk"), ("Wpk", "bpk")))
    a["w_v2"], a["w_pv"] = rows(g[n + "Wv"], g[n + "bv"]), rows(g[n + "Wpv"], g[n + "bpv"])
    w = rows(g[m + "qkv_w"], g[m + "qkv_b"])
    qk = np.zeros((D + 1, NJ, 2, 4, 32), f)
    qk[..., :HD] = w[:, :2 * D].reshape(D + 1, 2, NJ, 4, HD).transpose(0, 2, 1, 3, 4)[:, :, ::-1]
    qk[D, :, 0, :, HD] = -1.0
    a["w_qk"] = qk.reshape(D + 1, -1)
    a["w_v3"] = w[:, 2 * D:]
    proj = np.zeros((4, 32, NJ, D), f)
    proj[:, :HD] = g[m + "proj_w"].reshape(NJ, 4, HD, D).transpose(1, 2, 0, 3)
    proj[0, HD, 0] = g[m + "proj_b"]
    a["w_proj"] = proj.reshape(P, NJ, D)
    a["w_gate"] = g[m + "gate_w"].reshape(2, C, NE).transpose(1, 0, 2)
    sd = lambda x: x.reshape(NT, P, D).transpose(1, 0, 2).reshape(P, NT * D)
    a["ln1w"], a["ln1b"], a["ln2w"], a["ln2b"] = (sd(g[t + x]) for x in ("ln1_w", "ln1_b", "ln2_w", "ln2_b"))
    a["affine"] = np.stack([g[m + x] for x in ("ln1_g", "ln1_b", "ln2_g", "ln2_b")], 1).reshape(2, C, 4).transpose(1, 0, 2)
    a["e_b1"] = g[m + "b1"].reshape(NE, HC, P).transpose(0, 2, 1)
    a["e_b2"] = np.broadcast_to(g[m + "b2"][:, None], (NE, P, D))
    a["e_w1"] = g[m + "w1"].reshape(NE, 2, C, H).transpose(0, 2, 1, 3).reshape(NE, C, 2 * H)
    a["e_w2"] = g[m + "w2"].reshape(NE, HC, P, D).transpose(0, 2, 1, 3).reshape(NE, P, HC * D)
    return {k: np.ascontiguousarray(v) for k, v in a.items()}


def kernel(**inputs):
    import numpy as np
    import concourse.bacc as bacc
    from concourse.bass_utils import run_bass_kernel_spmd as run

    nc = bacc.Bacc("TRN2", target_bir_lowering=False, num_devices=1)
    arrays = layouts(np, {k: np.asarray(v) for k, v in inputs.items()})
    A = {k: nc.dram_tensor(f"in_{k}", v.shape, mybir.dt.from_np(v.dtype), kind="ExternalInput").ap() for k, v in arrays.items()}
    out = nc.dram_tensor("result", (B, S, D), mybir.dt.float32, kind="ExternalOutput").ap()
    block_kernel(nc, A, out)
    r = run(nc, [{f"in_{k}": v for k, v in arrays.items()}], core_ids=[0])
    return r.results[0]["result"]
```
